# Optimizing a Trainium2 kernel written in Bass

```python
import numpy as np
import jax
import jax.numpy as jnp

def _softmax(x, axis=-1):
    return jax.nn.softmax(x, axis=axis)

def _gelu(x):
    return jax.nn.gelu(x, approximate=True)

def _silu(x):
    return jax.nn.silu(x)

def _sigmoid(x):
    return jax.nn.sigmoid(x)

def _layernorm(x, axis=-1, eps=1e-05):
    m = jnp.mean(x, axis=axis, keepdims=True)
    v = jnp.var(x, axis=axis, keepdims=True)
    return (x - m) / jnp.sqrt(v + eps)

def _scatter_add(tgt, idx, src, axis=0):
    return tgt.at[idx].add(src)

def _segment_sum(src, seg, n):
    return jax.ops.segment_sum(src, seg, n)
kernel_name = 'mk_gps_d1_gnn_r8_030bc3'

def setup_inputs(seed: int=0):
    np.random.seed(seed)
    _w = jnp.asarray

    def _rec_inputs():
        import jax
        import jax.numpy as jnp
        _gk = jax.random.key(seed)
        x = -0.0001126 + 1 * jax.random.normal(jax.random.fold_in(_gk, 1), (3750, 256), jnp.float32)
        src = jax.random.randint(jax.random.fold_in(_gk, 2), (60000,), 0, 3750, jnp.int32)
        dst = jax.random.randint(jax.random.fold_in(_gk, 3), (60000,), 0, 3750, jnp.int32)
        _o = jnp.argsort(dst, stable=True)
        src = src[_o]
        dst = dst[_o]
        edge_type_8 = jax.random.randint(jax.random.fold_in(_gk, 12), (60000,), 0, 8, jnp.int32)
        return (x, src, dst, edge_type_8)
    x, src, dst, edge_type_8 = _rec_inputs()

    def _L0_gnn_setup():
        import jax, jax.numpy as jnp
        import numpy as np
        N_NODES = 3750
        N_EDGES = 60000
        IN_FEAT = 256
        OUT_FEAT = 256
        N_RELS = 8
        N_HEADS = 4
        HEAD_DIM = OUT_FEAT // N_HEADS
        LEAKY_SLOPE = 0.2
        key = jax.random.key(seed)
        ks = jax.random.split(key, 8)
        inputs = jax.random.normal(ks[0], (N_NODES, IN_FEAT), dtype=jnp.float32)
        conv_weights = jax.random.normal(ks[1], (N_RELS, N_HEADS, IN_FEAT, HEAD_DIM), dtype=jnp.float32) * (1.0 / np.sqrt(IN_FEAT))
        attn_l = jax.random.normal(ks[2], (N_RELS, N_HEADS, HEAD_DIM), dtype=jnp.float32) * 0.1
        attn_r = jax.random.normal(ks[3], (N_RELS, N_HEADS, HEAD_DIM), dtype=jnp.float32) * 0.1
        h_bias = jax.random.normal(ks[4], (OUT_FEAT,), dtype=jnp.float32) * 0.02
        edge_src = jax.random.randint(ks[5], (N_EDGES,), 0, N_NODES, dtype=jnp.int32)
        edge_dst = jax.random.randint(ks[6], (N_EDGES,), 0, N_NODES, dtype=jnp.int32)
        edge_type = jax.random.randint(ks[7], (N_EDGES,), 0, N_RELS, dtype=jnp.int32)
        return {'inputs': inputs, 'conv_weights': conv_weights, 'attn_l': attn_l, 'attn_r': attn_r, 'h_bias': h_bias, 'edge_src': edge_src, 'edge_dst': edge_dst, 'edge_type': edge_type}
    _L0_gnn_all = _L0_gnn_setup()
    _L0_gnn_in = {k: v for k, v in _L0_gnn_all.items() if k in ('conv_weights', 'attn_l', 'attn_r', 'h_bias')}
    del _L0_gnn_all

    def _L0_mix_setup():
        import jax, jax.numpy as jnp
        import numpy as np
        MIDC = 256
        HEADS = 8
        HEADC = MIDC // HEADS
        EPS = 1e-05

        def _ln(x, gamma, beta):
            mu = jnp.mean(x, axis=-1, keepdims=True)
            var = jnp.var(x, axis=-1, keepdims=True)
            return (x - mu) * jax.lax.rsqrt(var + EPS) * gamma + beta
        key = jax.random.key(seed)
        ks = jax.random.split(key, 8)
        B, HW, C = (8, 512, MIDC)
        s = 1.0 / np.sqrt(C)
        return {'x': jax.random.normal(ks[0], (B, HW, C), jnp.float32), 'w_qkv': jax.random.normal(ks[1], (C, 3 * C), jnp.float32) * s, 'b_qkv': jnp.zeros((3 * C,), jnp.float32), 'kln_g': jnp.ones((HEADC,), jnp.float32), 'kln_b': jnp.zeros((HEADC,), jnp.float32), 'vln_g': jnp.ones((HEADC,), jnp.float32), 'vln_b': jnp.zeros((HEADC,), jnp.float32), 'w1': jax.random.normal(ks[2], (C, C), jnp.float32) * s, 'b1': jnp.zeros((C,), jnp.float32), 'w2': jax.random.normal(ks[3], (C, C), jnp.float32) * s, 'b2': jnp.zeros((C,), jnp.float32)}
    _L0_mix_all = _L0_mix_setup()
    _L0_mix_in = {k: v for k, v in _L0_mix_all.items() if k in ('w_qkv', 'b_qkv', 'kln_g', 'kln_b', 'vln_g', 'vln_b', 'w1', 'b1', 'w2', 'b2')}
    del _L0_mix_all

    def _L0_ffn_setup():
        import jax, jax.numpy as jnp
        import numpy as np
        B, S, D = (8, 512, 256)
        H = 4 * D
        CAPACITY = 0.5
        key = jax.random.key(seed)
        ks = jax.random.split(key, 6)
        x = jax.random.normal(ks[0], (B, S, D), dtype=jnp.float32)
        attention_mask = jnp.zeros((B, 1, 1, S), dtype=jnp.float32)
        wr = jax.random.normal(ks[1], (D, 1), dtype=jnp.float32) * 0.02
        br = jnp.zeros((1,), dtype=jnp.float32)
        w1 = jax.random.normal(ks[2], (D, H), dtype=jnp.float32) * 0.02
        b1 = jnp.zeros((H,), dtype=jnp.float32)
        w2 = jax.random.normal(ks[3], (H, D), dtype=jnp.float32) * 0.02
        b2 = jnp.zeros((D,), dtype=jnp.float32)
        return {'x': x, 'attention_mask': attention_mask, 'wr': wr, 'br': br, 'w1': w1, 'b1': b1, 'w2': w2, 'b2': b2}
    _L0_ffn_all = _L0_ffn_setup()
    _L0_ffn_in = {k: v for k, v in _L0_ffn_all.items() if k in ('attention_mask', 'wr', 'br', 'w1', 'b1', 'w2', 'b2')}
    del _L0_ffn_all
    return {'x': x, 'src': src, 'dst': dst, 'edge_type_8': edge_type_8, 'L0_gnn_conv_weights': _L0_gnn_in['conv_weights'], 'L0_gnn_attn_l': _L0_gnn_in['attn_l'], 'L0_gnn_attn_r': _L0_gnn_in['attn_r'], 'L0_gnn_h_bias': _L0_gnn_in['h_bias'], 'L0_mix_w_qkv': _L0_mix_in['w_qkv'], 'L0_mix_b_qkv': _L0_mix_in['b_qkv'], 'L0_mix_kln_g': _L0_mix_in['kln_g'], 'L0_mix_kln_b': _L0_mix_in['kln_b'], 'L0_mix_vln_g': _L0_mix_in['vln_g'], 'L0_mix_vln_b': _L0_mix_in['vln_b'], 'L0_mix_w1': _L0_mix_in['w1'], 'L0_mix_b1': _L0_mix_in['b1'], 'L0_mix_w2': _L0_mix_in['w2'], 'L0_mix_b2': _L0_mix_in['b2'], 'L0_ffn_attention_mask': _L0_ffn_in['attention_mask'], 'L0_ffn_wr': _L0_ffn_in['wr'], 'L0_ffn_br': _L0_ffn_in['br'], 'L0_ffn_w1': _L0_ffn_in['w1'], 'L0_ffn_b1': _L0_ffn_in['b1'], 'L0_ffn_w2': _L0_ffn_in['w2'], 'L0_ffn_b2': _L0_ffn_in['b2']}

def reference(x, src, dst, edge_type_8, L0_gnn_conv_weights, L0_gnn_attn_l, L0_gnn_attn_r, L0_gnn_h_bias, L0_mix_w_qkv, L0_mix_b_qkv, L0_mix_kln_g, L0_mix_kln_b, L0_mix_vln_g, L0_mix_vln_b, L0_mix_w1, L0_mix_b1, L0_mix_w2, L0_mix_b2, L0_ffn_attention_mask, L0_ffn_wr, L0_ffn_br, L0_ffn_w1, L0_ffn_b1, L0_ffn_w2, L0_ffn_b2):
    import jax
    import jax.numpy as jnp

    def _L0_gnn_ref(inputs, conv_weights, attn_l, attn_r, h_bias, edge_src, edge_dst, edge_type):
        import jax, jax.numpy as jnp
        import numpy as np
        N_NODES = 3750
        N_EDGES = 60000
        IN_FEAT = 256
        OUT_FEAT = 256
        N_RELS = 8
        N_HEADS = 4
        HEAD_DIM = OUT_FEAT // N_HEADS
        LEAKY_SLOPE = 0.2
        feat_all = jnp.einsum('ni,rhid->rnhd', inputs, conv_weights)
        feat_src_e = feat_all[edge_type, edge_src]
        feat_dst_e = feat_all[edge_type, edge_dst]
        el = jnp.sum(feat_src_e * attn_l[edge_type], axis=-1)
        er = jnp.sum(feat_dst_e * attn_r[edge_type], axis=-1)
        e = jax.nn.leaky_relu(el + er, negative_slope=LEAKY_SLOPE)
        m = jax.ops.segment_max(e, edge_dst, num_segments=N_NODES)
        ex = jnp.exp(e - m[edge_dst])
        denom = jax.ops.segment_sum(ex, edge_dst, num_segments=N_NODES)
        alpha = ex / denom[edge_dst]
        h = jax.ops.segment_sum(alpha[..., None] * feat_src_e, edge_dst, num_segments=N_NODES)
        h = h.reshape(N_NODES, OUT_FEAT) + h_bias
        return h

    def _L0_mix_ref(x, w_qkv, b_qkv, kln_g, kln_b, vln_g, vln_b, w1, b1, w2, b2):
        import jax, jax.numpy as jnp
        import numpy as np
        MIDC = 256
        HEADS = 8
        HEADC = MIDC // HEADS
        EPS = 1e-05

        def _ln(x, gamma, beta):
            mu = jnp.mean(x, axis=-1, keepdims=True)
            var = jnp.var(x, axis=-1, keepdims=True)
            return (x - mu) * jax.lax.rsqrt(var + EPS) * gamma + beta
        B, HW, C = x.shape
        bias = x
        qkv = (x @ w_qkv + b_qkv).reshape(B, HW, HEADS, 3 * HEADC)
        qkv = qkv.transpose(0, 2, 1, 3)
        q, k, v = jnp.split(qkv, 3, axis=-1)
        k = _ln(k, kln_g, kln_b)
        v = _ln(v, vln_g, vln_b)
        kv = jnp.einsum('bhnd,bhne->bhde', k, v) / HW
        out = jnp.einsum('bhnd,bhde->bhne', q, kv)
        out = out.transpose(0, 2, 1, 3).reshape(B, HW, C)
        ret = out + bias
        h = jax.nn.gelu(ret @ w1 + b1, approximate=False)
        return h @ w2 + b2 + bias

    def _L0_ffn_ref(x, attention_mask, wr, br, w1, b1, w2, b2):
        import jax, jax.numpy as jnp
        import numpy as np
        B, S, D = (8, 512, 256)
        H = 4 * D
        CAPACITY = 0.5
        b, s, d = x.shape
        weights = (jnp.einsum('bsd,do->bso', x, wr) + br)[..., 0]
        k = max(1, int(CAPACITY * s))
        kk = k - 1 if k > 1 else 1
        _, idx = jax.lax.top_k(weights, k)
        sel_idx = idx[:, :kk]
        sel = jnp.take_along_axis(x, sel_idx[:, :, None], axis=1)
        h = jax.nn.gelu(jnp.einsum('bkd,dh->bkh', sel, w1) + b1)
        y = jnp.einsum('bkh,hd->bkd', h, w2) + b2
        w_sel = jnp.take_along_axis(weights, sel_idx, axis=1)
        y = y * w_sel[..., None]
        batch_idx = jnp.arange(b)[:, None]
        processed = jnp.zeros_like(x).at[batch_idx, sel_idx].set(y)
        return processed + x
    xn = _layernorm(x, axis=-1)
    x = x + _L0_gnn_ref(xn, L0_gnn_conv_weights, L0_gnn_attn_l, L0_gnn_attn_r, L0_gnn_h_bias, src, dst, edge_type_8) + _L0_mix_ref(xn[None], L0_mix_w_qkv, L0_mix_b_qkv, L0_mix_kln_g, L0_mix_kln_b, L0_mix_vln_g, L0_mix_vln_b, L0_mix_w1, L0_mix_b1, L0_mix_w2, L0_mix_b2)[0]
    x = x + _L0_ffn_ref(_layernorm(x, axis=-1)[None], L0_ffn_attention_mask, L0_ffn_wr, L0_ffn_br, L0_ffn_w1, L0_ffn_b1, L0_ffn_w2, L0_ffn_b2)[0]
    return x

_drawn_inputs = setup_inputs


def setup_inputs(seed=0):
    import zlib

    import numpy as np

    out = dict(_drawn_inputs(seed))
    spreads = {'L0_mix_b_qkv': (0.0, 0.1),
     'L0_mix_kln_g': (1.0, 0.6),
     'L0_mix_kln_b': (0.0, 0.452),
     'L0_mix_vln_g': (1.0, 0.592),
     'L0_mix_vln_b': (0.0, 0.401),
     'L0_mix_b1': (0.0, 0.1),
     'L0_mix_b2': (0.0, 0.1),
     'L0_ffn_b1': (0.0, 0.8),
     'L0_ffn_b2': (0.0, 0.8)}
    factors = {'L0_gnn_h_bias': 6.274, 'L0_ffn_wr': 5.632, 'L0_ffn_w1': 6.19, 'L0_ffn_w2': 5.811}
    for name, (base, spread) in spreads.items():
        noise = np.random.default_rng([zlib.crc32(name.encode()), seed]).standard_normal(out[name].shape)
        drawn = base * np.exp(spread * noise) if base else spread * noise
        out[name] = jnp.asarray(drawn.astype(out[name].dtype))
    for name, factor in factors.items():
        out[name] = (out[name] * factor).astype(out[name].dtype)
    return out
```

```python
from contextlib import ExitStack

import concourse.bass as bass
from concourse import mybir

F32 = mybir.dt.float32
BF16 = mybir.dt.bfloat16
I32 = mybir.dt.int32
ALU = mybir.AluOpType
ACT = mybir.ActivationFunctionType
AX = mybir.AxisListType
SUM = bass.bass_isa.ReduceOp.add

N, D = 3750, 256
P = 125
W = N // P
K = D // 128
R, H, HD = 8, 4, 64
HC = HD + 1
ROW = H * HC
E = 60000
J = 8
CH = P * J
NC = E // CH
U = 4
JV = 5
MH, MD = 8, 32
F = 4 * D
FC = F // 128
BLK = 3
NB = W // BLK
BN = BLK * P
TOPK = N // 2 - 1
EPS = 1e-5
NEG = -1e30
PARTS = ((0, 112), (112, P))
ROUNDS = ((25, 0), (18, 0), (12, 1), (6, 1), (0, 1))


def wait(eng, signal, value):
    if not isinstance(value, int) or value > 0:
        eng.wait_ge(signal, value)


class Steps:

    def __init__(self, eng, counter, settle=None):
        self.eng, self.counter, self.base, self.k, self.settle = eng, counter, 0, 0, settle

    def at(self, base):
        self.base, self.k = base, 0

    def __call__(self, ins):
        self.k += 1
        ins.then_inc(self.counter, 1)
        self.eng.wait_ge(self.counter, self.base + self.k)
        if self.settle and not isinstance(self.base, int):
            self.settle(self.eng)


def reverse(ap):
    part, (step, n) = ap.ap
    return bass.AP(ap.tensor, ap.offset + step * (n - 1), [part, (-step, n)])


def graph_layer(nc, a, out):
    with ExitStack() as ctx:
        def sb(name, shape, dt=F32):
            return ctx.enter_context(nc.sbuf_tensor(name, shape, dt))

        def sem(name):
            return ctx.enter_context(nc.semaphore(name))

        table = nc.dram_tensor("feature_table", (N * R, ROW), F32).ap()
        dst_first = nc.dram_tensor("dst_of_chunks", (1, NC), I32).ap()
        dst_pad = nc.dram_tensor("dst_padded", (1, E + 2), I32).ap()

        x_sb = sb("x_sb", [128, W, D])
        xnT = sb("xnT", [128, K, N])
        acc = sb("acc", [128, W, ROW])
        ring = sb("ring", [128, U, J, ROW])
        waug = sb("waug", [128, K, R, ROW])
        arena = sb("arena", [128, 6000])
        masks = sb("masks", [128, 7680], BF16)
        wer = sb("wer", [128, K, R * H])
        w1m = sb("w1m", [128, K, D])
        w2m = sb("w2m", [128, K, D])
        bkv = sb("bkv", [1, 2 * D])
        bq = sb("bq", [128, K])
        b1m = sb("b1m", [128, K])
        beff = sb("beff", [128, K])
        b1f = sb("b1f", [128, FC])
        wr = sb("wr", [128, K])
        br = sb("br", [1, 1])
        bias_rows = sb("bias_rows", [128, 3, D])
        ident = sb("ident", [128, 128])
        headmask = sb("headmask", [128, 128])
        ones = sb("ones", [128, 128])
        iota = sb("iota", [128, P])
        nodecol = sb("nodecol", [128, W])
        wbase = sb("wbase", [128, W])
        stats = sb("stats", [128, BLK, 6])
        mv2 = sb("mv2", [128, BLK, 2])
        mv = sb("mv", [128, W, 2])
        rstd = sb("rstd", [128, W])
        epsc = sb("epsc", [128, 1])
        var16 = sb("var16", [128, 2, 2 * MH])
        xn_t = sb("xn_t", [128, BLK, D])
        xnT_s = sb("xnT_s", [128, 2, K, P])
        er_sb = sb("er_sb", [128, W * R * H])
        dstf = sb("dstf", [128, NC, J + 2])
        row_idx = sb("row_idx", [128, NC, J], I32)
        idx_now = sb("idx_now", [128, U, J], I32)
        penA = sb("penA", [128, NC, J], BF16)
        penZ = sb("penZ", [128, NC, J], BF16)
        pen0 = sb("pen0", [128, NC, H])
        pen1 = sb("pen1", [128, NC, H])
        dfirstf = sb("dfirstf", [128, NC])
        hi = sb("hi", [1, NC + 1], I32)
        sentinel = sb("sentinel", [1, 1], I32)
        fac = sb("fac", [4, 3])
        facdiag = sb("facdiag", [4, 4])
        pens_now = sb("pens_now", [128, U, 2, H])
        eqc = sb("eqc", [128, 1])
        fsc = sb("fsc", [128, H])
        pcol = sb("pcol", [128, 1], I32)
        pcolf = sb("pcolf", [128, 1])
        psh = sb("psh", [128, len(ROUNDS)], I32)
        pmask = sb("pmask", [128, 2])
        prefix = sb("prefix", [128, 1], I32)
        cand = sb("cand", [128, 3], I32)
        count = sb("count", [128, 4])
        picked = sb("picked", [128, 1], I32)

        banks = []
        for i in range(4):
            pair = ctx.enter_context(nc.psum_tensor(f"bank{2 * i}", [128, 2, 512], F32))
            banks += [pair[:, 0, :], pair[:, 1, :]]
            if i == 1:
                feat_ps = [pair[:, :, 0:ROW]]
            if i == 2:
                feat_ps.append(pair[:, :, 0:ROW])

        flat_acc = acc[:, :, :].rearrange("p w c -> p (w c)")
        attn_b = [flat_acc[:, i * R * D:(i + 1) * R * D].rearrange("p (q d) -> p q d", d=HD) for i in range(2)]
        attn_prod = flat_acc[:, 2 * R * D:3 * R * D].rearrange("p (q d) -> p q d", d=HD)
        sq = flat_acc[:, 6144:6144 + 2 * D]
        typ_t = flat_acc[:, 6660:7140].bitcast(I32).rearrange("p (c j) -> p c j", j=J)
        src_t = flat_acc[:, 7140:7620].bitcast(I32).rearrange("p (c j) -> p c j", j=J)
        dfirst = flat_acc[:, 7620:7620 + NC].bitcast(I32)
        dlast = flat_acc[0:1, 7680:7680 + NC].bitcast(I32)
        dlastf = flat_acc[0:1, 7740:7740 + NC]
        hi_f = flat_acc[0:1, 3600:3600 + NC + 1]
        pen = flat_acc[:, 0:NC * (J + 1)].rearrange("p (c j) -> p c j", j=J + 1)
        scanp = flat_acc[:, 600:600 + 2 * NC * J].rearrange("p (s c j) -> p s c j", s=2, j=J)
        hi_cmp = flat_acc[0:1, 1600:1600 + NC * W].rearrange("p (c w) -> p c w", w=W)
        dst10 = xnT[:, 0, 0:NC * (J + 2)].bitcast(I32).rearrange("p (c j) -> p c j", j=J + 2)
        stage = [ring[:, u, :, :] for u in range(2)]
        flat_ring = ring[:, :, :, :].rearrange("p u j c -> p (u j c)")
        hT_f = [flat_ring[:, i * FC * BN:(i + 1) * FC * BN].rearrange("p (f n) -> p f n", f=FC) for i in range(2)]
        flat_waug = waug[:, :, :, :].rearrange("p k r c -> p (k r c)")
        w1f = flat_waug[:, 0:K * F].rearrange("p (k f) -> p k f", k=K)
        w2f = flat_waug[:, K * F:K * F + FC * D].rearrange("p (f n) -> p f n", f=FC)

        flat_xnT = xnT[:, :, :].rearrange("p k n -> p (k n)")
        taken = [0]

        def scratch(*shape, parts=128):
            size = 1
            for n in shape:
                size *= n
            taken[0] += size
            part = flat_xnT[0:parts, taken[0] - size:taken[0]]
            names = "abc"[:len(shape)]
            return part.rearrange(f"p ({' '.join(names)}) -> p {' '.join(names)}", **dict(zip(names, shape)))

        dloc = scratch(2, J)
        ersel = scratch(J, H, R)
        er_e = scratch(J, H)
        score = scratch(H, J)
        e_cur = scratch(2, H, J)
        runF = scratch(2, H, J)
        runB = scratch(2, H, J)
        cmx = scratch(3, H, J)
        diff = scratch(2, H, J)
        ex = scratch(U, H, J)
        penT = scratch(2, 2 * P, parts=4)
        gx = scratch(2, P + 1, parts=4)
        hx = scratch(2, P + 1, parts=4)
        wst = flat_ring[0:1, 2 * FC * BN:2 * FC * BN + 2 * BN].rearrange("p (u n) -> p u n", u=2)

        spare = flat_ring[:, 2 * FC * BN + 2 * BN:]
        rden = spare[:, 0:W * H].rearrange("p (w h) -> p w h", h=H)
        wcol, wsel = (spare[:, (H + i) * W:(H + 1 + i) * W] for i in range(2))
        tie = spare[:, (H + 2) * W:(H + 4) * W].rearrange("p (i w) -> p i w", w=W)

        def words(lo, n, k):
            return arena[:, lo:lo + n * k].rearrange("p (k n) -> p k n", k=k)

        wqkv = words(0, 3 * D, K)
        wkv = words(1536, 2 * D, K)
        gam = arena[:, 2560:3072]
        bet = arena[:, 3072:3584]
        kv_s = words(3584, 2 * D, 2)
        q_packed = words(3584, D, K)
        brow = arena[0:1, 4608:5376]
        wqT = words(5376, D, K)
        kvd = words(1536, 128, K)
        mixT = words(1792, D, K)
        cvec = arena[:, 2304:2304 + K]
        weff = words(2560, D, K)
        hT_m = [words(3072 + i * K * BN, BN, K) for i in range(2)]
        dst_row = [arena[:, i * CH:(i + 1) * CH].bitcast(I32) for i in range(2)]
        dhot = [arena[:, (2 + i) * CH:(3 + i) * CH] for i in range(2)]
        ehot = [words((4 + i) * CH, P, J) for i in range(2)]
        wall = arena[:, 0:N]
        at_limit = masks[:, 0:2 * N].bitcast(F32)
        count_out = arena[:, N:N + N // 2].bitcast(BF16)
        rel_hot = masks[:, 0:3840].rearrange("p (c j r) -> p c j r", j=J, r=R)
        penF = masks[:, 3840:5760].rearrange("p (c h j) -> p c h j", h=H, j=J)
        penB = masks[:, 5760:7680].rearrange("p (c h j) -> p c h j", h=H, j=J)

        def dram(ap, offset, pattern):
            return bass.AP(ap.tensor, offset, pattern)

        x_loaded = [sem(f"x_loaded{g}") for g in range(3)]
        dst_copied = sem("dst_copied")
        first_copied = sem("first_copied")
        edges_loaded = sem("edges_loaded")
        idx_loaded = sem("idx_loaded")
        conv_loaded = sem("conv_loaded")
        attn_loaded = sem("attn_loaded")
        qkv_loaded = sem("qkv_loaded")
        mixw_loaded = sem("mixw_loaded")
        rows_loaded = sem("rows_loaded")
        ffnw_loaded = sem("ffnw_loaded")
        pool_step = sem("pool_step")
        consts_ready = sem("consts_ready")
        vector_step = sem("vector_step")
        var_ready = sem("var_ready")
        std_ready = sem("std_ready")
        weights_ready = sem("weights_ready")
        idx_ready = sem("idx_ready")
        xn_ready = sem("xn_ready")
        xn_turned = sem("xn_turned")
        xn_added = sem("xn_added")
        xnT_ready = sem("xnT_ready")
        xnT_kept = sem("xnT_kept")
        feat_even_done = sem("feat_even_done")
        feat_odd_done = sem("feat_odd_done")
        feat_even_out = sem("feat_even_out")
        feat_odd_out = sem("feat_odd_out")
        table_written = [sem(f"table_written{u}") for u in range(2)]
        kv_done = sem("kv_done")
        er_done = sem("er_done")
        er_out = sem("er_out")
        sq_ready = sem("sq_ready")
        kvar_ready = sem("kvar_ready")
        kstd_ready = sem("kstd_ready")
        krstd_ready = sem("krstd_ready")
        kv_normed = sem("kv_normed")
        kv_scaled = sem("kv_scaled")
        kv_summed = sem("kv_summed")
        wq_turned = sem("wq_turned")
        wqT_ready = sem("wqT_ready")
        fold_mm = sem("fold_mm")
        fold_ready = sem("fold_ready")
        masks_ready = sem("masks_ready")
        mix_h = sem("mix_h")
        mix_gelu = sem("mix_gelu")
        mix_out = sem("mix_out")
        mix_added = sem("mix_added")
        idx_copied = sem("idx_copied")
        gathered = [sem(f"gathered{u}") for u in range(U)]
        dst_row_loaded = [sem(f"dst_row_loaded{v}") for v in range(2)]
        dhot_first = sem("dhot_first")
        dhot_further = sem("dhot_further")
        er_first = sem("er_first")
        er_further = sem("er_further")
        er_used = sem("er_used")
        score_step = sem("score_step")
        scores_done = sem("scores_done")
        pens_turned = sem("pens_turned")
        pens_copied = sem("pens_copied")
        pens_staged = sem("pens_staged")
        runs_ready = sem("runs_ready")
        tails_turned = sem("tails_turned")
        carried = sem("carried")
        carry_step = sem("carry_step")
        fac_diff = sem("fac_diff")
        fac_exp = sem("fac_exp")
        facdiag_ready = sem("facdiag_ready")
        fac_spread = sem("fac_spread")
        carry_back = sem("carry_back")
        weight_step = sem("weight_step")
        diff_ready = sem("diff_ready")
        ex_ready = sem("ex_ready")
        scaled_vector = sem("scaled_vector")
        scaled_scalar = sem("scaled_scalar")
        place_step = sem("place_step")
        place_further_step = sem("place_further_step")
        ehot_first = sem("ehot_first")
        ehot_further = sem("ehot_further")
        acc_rescaled = sem("acc_rescaled")
        sum_first = sem("sum_first")
        sum_further = sem("sum_further")
        kept_first = sem("kept_first")
        kept_further = sem("kept_further")
        x2_step = sem("x2_step")
        x2_var = sem("x2_var")
        x2_std = sem("x2_std")
        x2_rstd = sem("x2_rstd")
        y_ready = sem("y_ready")
        y_turned = sem("y_turned")
        y_added = sem("y_added")
        yT_ready = sem("yT_ready")
        gate_row = sem("gate_row")
        gate_kept = sem("gate_kept")
        gate_spread = sem("gate_spread")
        gate_out = sem("gate_out")
        ffn_h = sem("ffn_h")
        ffn_gelu = sem("ffn_gelu")
        ffn_z = sem("ffn_z")
        ffn_z_out = sem("ffn_z_out")
        ffn_z_bias = sem("ffn_z_bias")
        topk_step = sem("topk_step")
        flag_ready = sem("flag_ready")
        flag_summed = sem("flag_summed")
        rows_done = sem("rows_done")
        settled = sem("settled")
        out_written = sem("out_written")

        block = ctx.enter_context(nc.Block())

        def settle(eng):
            eng.sem_inc(settled, 1)

        def chunks(eng, body):
            for u in range(U):
                body(u, 0, u)
            with eng.Fori(1, NC // U - 1) as n:
                for u in range(U):
                    body(n * U + u, n, u)
            for u in range(U):
                body(NC - U + u, NC // U - 1, u)

        def ffn_pairs(eng, hidden, rows):
            hidden(0, 0)

            def pair(i, last=False):
                hidden(2 * i + 1, 1)
                rows(2 * i, 0)
                if not last:
                    hidden(2 * i + 2, 0)
                rows(2 * i + 1, 1)

            pair(0)
            with eng.Fori(1, NB // 2 - 1) as i:
                pair(i)
            pair(NB // 2 - 1, last=True)

        def span(eng, c):
            lo = eng.value_load(hi[0:1, bass.ds(c, 1)], min_val=0, max_val=W - 1)
            up = eng.value_load(hi[0:1, bass.ds(c + 1, 1)], min_val=0, max_val=W - 1)
            return lo, up

        def further(eng, lo, up, body):
            with eng.If(lo < up):
                with eng.Fori(lo + 1, up + 1) as w:
                    body(w)

        @block.sync
        def _(sp):
            for g in range(3):
                for p0, p1 in PARTS:
                    sp.dma_start(x_sb[p0:p1, 10 * g:10 * g + 10, :],
                                 a["x"].rearrange("(w p) d -> p w d", p=P)[p0:p1, 10 * g:10 * g + 10, :])\
                      .then_inc(x_loaded[g], 16)
            sp.dma_start(dram(dst_pad, 1, [[N, 16], [1, N]]), dram(a["dst"], 0, [[N, 16], [1, N]])).then_inc(dst_copied, 16)
            sp.wait_ge(consts_ready, 1)
            for at in (0, E + 1):
                sp.dma_start(dst_pad[0:1, at:at + 1], sentinel[:, :]).then_inc(dst_copied, 16)
            for ap, to in ((a["src"], src_t), (a["edge_type_8"], typ_t)):
                sp.dma_start(to[0:P], dram(ap, 0, [[J, P], [CH, NC], [1, J]])).then_inc(idx_loaded, 16)
            sp.wait_ge(dst_copied, 48)
            sp.dma_start(dst10[0:P], dram(dst_pad, 0, [[J, P], [CH, NC], [1, J + 2]])).then_inc(edges_loaded, 16)
            sp.dma_start(dlast, dram(dst_pad, CH, [[0, 1], [CH, NC]]), allow_slow_non_contiguous=True).then_inc(edges_loaded, 16)
            sp.dma_start(dst_first, dram(dst_pad, 1, [[0, 1], [CH, NC]]), allow_slow_non_contiguous=True).then_inc(first_copied, 16)
            sp.wait_ge(first_copied, 16)
            sp.dma_start(dfirst[0:P], dram(dst_first, 0, [[0, P], [1, NC]])).then_inc(edges_loaded, 16)

            def write_table(i):
                for u in range(2):
                    t = 2 * i + u
                    sp.wait_ge(feat_even_out, 2 * t + 2)
                    sp.wait_ge(feat_odd_out, 2 * t + 2)
                    for p0, p1 in PARTS:
                        sp.dma_start(
                            table[bass.ds(t * P * R + p0 * R, (p1 - p0) * R), :].rearrange("(p r) c -> p r c", r=R),
                            stage[u][p0:p1]).then_inc(table_written[u], 16)

            with sp.Fori(0, W // 2) as i:
                write_table(i)

            sp.wait_ge(feat_even_done, 2 * W)
            sp.wait_ge(feat_odd_done, 2 * W)
            sp.wait_ge(er_done, W)
            sp.dma_start(w1f, a["L0_ffn_w1"].rearrange("(k p) f -> p k f", p=128)).then_inc(ffnw_loaded, 16)
            sp.dma_start(w2f, a["L0_ffn_w2"].rearrange("(f p) n -> p f n", p=128)).then_inc(ffnw_loaded, 16)

            sp.wait_ge(mix_added, W)

            def load_dst_row(c, n, u):
                wait(sp, scores_done, c - 1)
                sp.dma_start(dst_row[u % 2], dram(dst_pad, c * CH + 1, [[0, 128], [1, CH]]))\
                  .then_inc(dst_row_loaded[u % 2], 16)

            chunks(sp, load_dst_row)

            with sp.Fori(0, NB) as b:
                sp.wait_ge(rows_done, b * BLK + BLK)
                for p0, p1 in PARTS:
                    sp.dma_start(out[bass.ds(b * BN, BN), :].rearrange("(w p) d -> p w d", p=P)[p0:p1],
                                 acc[p0:p1, bass.ds(b * BLK, BLK), 0:D]).then_inc(out_written, 16)
            sp.wait_ge(out_written, 32 * NB)

        @block.gpsimd
        def _(pool):
            own = Steps(pool, pool_step, settle)
            g = nc.gpsimd
            g.memset(sentinel[:, :], -1).then_inc(consts_ready, 1)
            g.memset(epsc[:, :], EPS)
            g.memset(ones[:, :], 1.0)
            g.memset(ident[:, :], 0.0)
            g.memset(kv_s[:, 1, :], 0.0)
            g.iota(iota[:, :], [[1, P]], base=0, channel_multiplier=0, allow_small_or_imprecise_dtypes=True)
            g.iota(nodecol[:, :], [[P, W]], base=0, channel_multiplier=1, allow_small_or_imprecise_dtypes=True)
            g.iota(wbase[:, :], [[P, W]], base=0, channel_multiplier=0, allow_small_or_imprecise_dtypes=True)
            g.iota(pcolf[:, :], [[0, 1]], base=0, channel_multiplier=1, allow_small_or_imprecise_dtypes=True)
            own(g.iota(pcol[:, :], [[0, 1]], base=0, channel_multiplier=1))
            own(g.affine_select(out=ident[:, :], in_=ident[:, :], compare_op=ALU.not_equal, fill=1.0,
                                base=0, pattern=[[-1, 128]], channel_multiplier=1))
            pool.wait_ge(rows_loaded, 16 * 7)
            g.tensor_tensor(bias_rows[0:P, 0, :], bias_rows[0:P, 0, :], bias_rows[0:P, 1, :], ALU.add)\
             .then_inc(consts_ready, 1)
            pool.wait_ge(consts_ready, 2)

            def window_pair(i):
                for u in range(2):
                    t = 2 * i + u
                    rows = x_sb[0:P, bass.ds(t, 1), :].rearrange("p w d -> p (w d)")
                    pool.wait_ge(xn_ready, t + 1)
                    settle(pool)
                    own.at(2 + 3 * t)
                    own(g.tensor_tensor(rows, rows, xn_t[0:P, u, :], ALU.add))
                    g.tensor_tensor(rows, rows, bias_rows[0:P, 0, :], ALU.add).then_inc(xn_added, 1)
                    pool.wait_ge(xnT_ready, t + 1)
                    settle(pool)
                    g.tensor_copy(xnT[:, :, bass.ds(t * P, P)], xnT_s[:, u, :, :]).then_inc(xnT_kept, 1)
                    pool.wait_ge(kv_normed, t + 1)
                    own(g.tensor_tensor(kv_s[0:P, u, :], kv_s[0:P, u, :], gam[0:P, :], ALU.mult))
                    own(g.tensor_tensor(kv_s[0:P, u, :], kv_s[0:P, u, :], bet[0:P, :], ALU.add))
                    g.sem_inc(kv_scaled, 1)

            with pool.Fori(0, W // 2) as i:
                window_pair(i)

            pool.wait_ge(idx_ready, 1)
            pool.wait_ge(masks_ready, 1)
            for u in range(2):
                pool.wait_ge(table_written[u], 32 * (W // 2))

            def gather(c, n, u):
                if not isinstance(c, int) or c >= U:
                    pool.wait_ge(sum_first, c - U + 1)
                    up = pool.value_load(hi[0:1, bass.ds(c - U + 1, 1)], min_val=0, max_val=W - 1)
                    pool.wait_ge(sum_further, up + 1)
                    settle(pool)
                g.tensor_copy(idx_now[0:P, u, :], row_idx[0:P, bass.ds(c, 1), :].rearrange("p c j -> p (c j)"))\
                 .then_inc(idx_copied, 1)
                for q, p in enumerate((pen0, pen1)):
                    ins = g.tensor_copy(pens_now[0:P, u, q, :], p[0:P, bass.ds(c, 1), :].rearrange("p c h -> p (c h)"))
                ins.then_inc(pens_staged, 1)
                pool.wait_ge(idx_copied, c + 1)
                settle(pool)
                for j in range(J):
                    g.indirect_dma_start(ring[0:P, u, j, :], None, table,
                                         bass.IndirectOffsetOnAxis(ap=idx_now[0:P, u, j:j + 1], axis=0))\
                     .then_inc(gathered[u], 16)

            chunks(pool, gather)

            def add_y(b):
                for i in range(BLK):
                    t = b * BLK + i
                    pool.wait_ge(y_ready, t + 1)
                    settle(pool)
                    rows = x_sb[0:P, bass.ds(t, 1), :].rearrange("p w d -> p (w d)")
                    g.tensor_tensor(rows, rows, xn_t[0:P, i, :], ALU.add).then_inc(y_added, 1)

            with pool.Fori(0, NB) as b:
                add_y(b)

            for r in range(len(ROUNDS)):
                pool.wait_ge(flag_ready, r + 1)
                g.partition_all_reduce(count[:, 1:2], count[:, 0:1], 128, SUM).then_inc(flag_summed, 1)

            with pool.Fori(0, W) as t:
                pool.wait_ge(ffn_z_out, t + 1)
                settle(pool)
                rows = acc[0:P, bass.ds(t, 1), 0:D].rearrange("p w d -> p (w d)")
                g.tensor_tensor(rows, rows, bias_rows[0:P, 2, :], ALU.add).then_inc(ffn_z_bias, 1)

        @block.scalar
        def _(act):
            s = nc.scalar
            for k in range(K):
                act.dma_start(waug[:, k, :, :].rearrange("p r (h c) -> p (r h) c", c=HC)[:, :, 0:HD],
                              dram(a["L0_gnn_conv_weights"], k * 128 * HD, [[HD, 128], [D * HD, R * H], [1, HD]]))\
                   .then_inc(conv_loaded, 16)
            act.dma_start(wqkv, a["L0_mix_w_qkv"].rearrange("(k p) n -> p k n", p=128)).then_inc(qkv_loaded, 16)
            act.dma_start(brow, dram(a["L0_mix_b_qkv"], 0, [[0, 1], [1, 3 * D]])).then_inc(qkv_loaded, 16)
            for i, name in enumerate(("L0_gnn_attn_l", "L0_gnn_attn_r")):
                act.dma_start(attn_b[i].rearrange("p q d -> p (q d)"), dram(a[name], 0, [[0, 128], [1, R * D]]))\
                   .then_inc(attn_loaded, 16)
            for to, gain, lo in ((gam, "L0_mix_kln_g", 0), (gam, "L0_mix_vln_g", D),
                                 (bet, "L0_mix_kln_b", 0), (bet, "L0_mix_vln_b", D)):
                act.dma_start(to[:, lo:lo + D].rearrange("p (h d) -> p h d", d=MD),
                              dram(a[gain], 0, [[0, 128], [0, MH], [1, MD]])).then_inc(rows_loaded, 16)
            for i, name in enumerate(("L0_gnn_h_bias", "L0_mix_b2", "L0_ffn_b2")):
                act.dma_start(bias_rows[:, i, :], dram(a[name], 0, [[0, 128], [1, D]])).then_inc(rows_loaded, 16)
            act.dma_start(w1m[:, :, :], a["L0_mix_w1"].rearrange("(k p) n -> p k n", p=128)).then_inc(mixw_loaded, 16)
            act.dma_start(w2m[:, :, :], a["L0_mix_w2"].rearrange("(k p) n -> p k n", p=128)).then_inc(mixw_loaded, 16)
            for h in range(MH):
                act.dma_start(bq[h % 4 * MD:(h % 4 + 1) * MD, h // 4:h // 4 + 1],
                              dram(a["L0_mix_b_qkv"], h * 3 * MD, [[1, MD], [1, 1]])).then_inc(mixw_loaded, 16)
            for to, name, n in ((b1m, "L0_mix_b1", K), (b1f, "L0_ffn_b1", FC), (wr, "L0_ffn_wr", K)):
                for k in range(n):
                    act.dma_start(to[:, k:k + 1], dram(a[name], k * 128, [[1, 128], [1, 1]])).then_inc(mixw_loaded, 16)
            act.dma_start(br[:, :], dram(a["L0_ffn_br"], 0, [[1, 1], [1, 1]])).then_inc(mixw_loaded, 16)

            act.wait_ge(var_ready, 1)
            s.activation(rstd[0:P, :], mv[0:P, :, 1], ACT.Sqrt, bias=epsc[0:P, :]).then_inc(std_ready, 1)
            act.wait_ge(wq_turned, 1)
            s.activation(wqT, banks[7].rearrange("p (k n) -> p k n", k=K), ACT.Copy).then_inc(wqT_ready, 1)

            def turned(t, u):
                act.wait_ge(xn_turned, t + 1)
                if not isinstance(t, int) or t >= 2:
                    act.wait_ge(er_done, t - 1)
                    act.wait_ge(xnT_kept, t - 1)
                s.activation(xnT_s[:, u, :, :], banks[u][:, 0:K * P].rearrange("p (k n) -> p k n", k=K),
                             ACT.Copy).then_inc(xnT_ready, 1)

            def feat_even(t, u, q):
                act.wait_ge(feat_even_done, 2 * t + q + 1)
                s.activation(stage[u][0:P, 4 * q:4 * q + 2, :], feat_ps[0][0:P], ACT.Copy).then_inc(feat_even_out, 1)

            def window_pair_act(i, last=False):
                for u in range(2):
                    t = 2 * i + u
                    wait(act, table_written[u], 32 * i)
                    feat_even(t, u, 0)
                    feat_even(t, u, 1)
                    act.wait_ge(kv_done, t + 1)
                    wait(act, kvar_ready, t)
                    s.activation(sq[0:P], banks[6][0:P, :], ACT.Square).then_inc(sq_ready, 1)
                    act.wait_ge(kvar_ready, t + 1)
                    s.activation(var16[0:P, 1, :], var16[0:P, 0, :], ACT.Sqrt, bias=epsc[0:P, :], scale=1.0 / MD)\
                     .then_inc(kstd_ready, 1)
                    if not last:
                        turned(t + 2, u)

            turned(0, 0)
            turned(1, 1)
            window_pair_act(0)
            with act.Fori(1, W // 2 - 1) as i:
                window_pair_act(i)
            window_pair_act(W // 2 - 1, last=True)

            act.wait_ge(fold_ready, 4)

            def mix_hidden(b, u):
                for k in range(K):
                    act.wait_ge(mix_h, b * K + k + 1)
                    if k == 0 and (not isinstance(b, int) or b >= 2):
                        act.wait_ge(mix_out, (b - 1) * BLK)
                    s.activation(hT_m[u][:, k, :], banks[u * K + k][:, 0:BN], ACT.Gelu, bias=beff[:, k:k + 1])\
                     .then_inc(mix_gelu, 1)

            for u in range(2):
                mix_hidden(u, u)
            with act.Fori(1, NB // 2) as i:
                for u in range(2):
                    mix_hidden(2 * i + u, u)

            act.sem_inc(kept_further, 1)

            def copy_pens(c, n, u):
                act.wait_ge(pens_turned, c + 1)
                wait(act, carried, 2 * (c - 1))
                s.activation(penT[:, u % 2, :], banks[2 + u % 2][0:4, 2 * P:4 * P], ACT.Copy).then_inc(pens_copied, 1)

            def keep(c):
                lo, up = span(act, c)
                act.wait_ge(sum_first, c + 1)
                s.activation(acc[0:P, bass.ds(lo, 1), :].rearrange("p w c -> p (w c)"), banks[6][0:P, 0:ROW], ACT.Copy)\
                 .then_inc(kept_first, 1)

                def keep_further(w):
                    act.wait_ge(sum_further, w + 1)
                    s.activation(acc[0:P, bass.ds(w, 1), :].rearrange("p w c -> p (w c)"), banks[7][0:P, 0:ROW],
                                 ACT.Copy).then_inc(kept_further, 1)

                further(act, lo, up, keep_further)

            def chunk_act(c, n, u):
                copy_pens(c, n, u)
                act.wait_ge(fac_diff, c + 1)
                s.activation(fac[:, 2:3], fac[:, 1:2], ACT.Exp).then_inc(fac_exp, 1)
                if not isinstance(c, int) or c >= 1:
                    keep(c - 1)
                act.wait_ge(diff_ready, c + 1)
                if not isinstance(c, int) or c >= U:
                    act.wait_ge(scaled_vector, c - U + 1)
                s.activation(ex[0:P, u], diff[0:P, u % 2], ACT.Exp).then_inc(ex_ready, 1)
                act.wait_ge(ex_ready, c + 1)
                for j in range(JV, J):
                    for h in range(H):
                        part = ring[0:P, u, j, h * HC:(h + 1) * HC]
                        s.activation(part, part, ACT.Copy, scale=ex[0:P, u, h, j:j + 1]).then_inc(scaled_scalar, 1)

            chunks(act, chunk_act)
            keep(NC - 1)

            act.wait_ge(x2_var, 1)
            s.activation(rstd[0:P, :], mv[0:P, :, 1], ACT.Sqrt, bias=epsc[0:P, :]).then_inc(x2_std, 1)

            def y_block(b, u):
                for i in range(BLK):
                    t = b * BLK + i
                    act.wait_ge(y_turned, t + 1)
                    s.activation(xnT[:, :, bass.ds(t * P, P)],
                                 banks[u * BLK + i][:, 0:K * P].rearrange("p (k n) -> p k n", k=K), ACT.Copy)\
                     .then_inc(yT_ready, 1)
                act.wait_ge(gate_row, b + 1)
                if not isinstance(b, int) or b >= 2:
                    act.wait_ge(gate_spread, b - 1)
                s.activation(wst[:, u, :], banks[6 + u][0:1, 0:BN], ACT.Identity, bias=br[:, :]).then_inc(gate_kept, 1)

            for u in range(2):
                y_block(u, u)
            with act.Fori(1, NB // 2) as i:
                for u in range(2):
                    y_block(2 * i + u, u)

            def ffn_gelus(b, u):
                for f in range(FC):
                    act.wait_ge(ffn_h, b * FC + f + 1)
                    if f == 0 and (not isinstance(b, int) or b >= 2):
                        act.wait_ge(ffn_z, (b - 1) * BLK)
                    s.activation(hT_f[u][:, f, :], banks[f % 4][:, 0:BN], ACT.Gelu_apprx_tanh, bias=b1f[:, f:f + 1])\
                     .then_inc(ffn_gelu, 1)

            def ffn_rows(b, u):
                for i in range(BLK):
                    t = b * BLK + i
                    act.wait_ge(ffn_z, t + 1)
                    s.activation(acc[0:P, bass.ds(t, 1), 0:D].rearrange("p w d -> p (w d)"),
                                 banks[4 + (u * BLK + i) % 2][0:P, 0:D], ACT.Copy).then_inc(ffn_z_out, 1)

            ffn_pairs(act, ffn_gelus, ffn_rows)

        @block.tensor
        def _(pe):
            mm = nc.tensor.matmul
            turn = nc.tensor.transpose

            pe.wait_ge(consts_ready, 2)
            pe.wait_ge(weights_ready, 1)
            for k in range(K):
                for hb in range(K):
                    ins = turn(banks[7][:, hb * D + k * 128:hb * D + (k + 1) * 128],
                               q_packed[:, k, hb * 128:(hb + 1) * 128], ident[:, :])
            ins.then_inc(wq_turned, 1)
            pe.wait_ge(wqT_ready, 1)

            def turn_window(t, u):
                pe.wait_ge(xn_ready, t + 1)
                if not isinstance(t, int) or t >= 2:
                    pe.wait_ge(xnT_ready, t - 1)
                    pe.wait_ge(er_out, t - 1)
                for k in range(K):
                    ins = turn(banks[u][:, k * P:(k + 1) * P], xn_t[0:P, u, k * 128:(k + 1) * 128], ident[0:P, 0:P])
                ins.then_inc(xn_turned, 1)

            def window(t, u):
                pe.wait_ge(xnT_ready, t + 1)
                for q in range(R // 2):
                    done, taken = ((feat_even_done, feat_even_out), (feat_odd_done, feat_odd_out))[q % 2]
                    wait(pe, taken, 2 * t + q // 2)
                    for r in range(2):
                        for k in range(K):
                            ins = mm(feat_ps[q % 2][0:P, r, :], xnT_s[:, u, k, :], waug[:, k, 2 * q + r, :],
                                     start=(k == 0), stop=(k == K - 1))
                    ins.then_inc(done, 1)
                wait(pe, kv_normed, t)
                mm(banks[6][0:P, :], ones[0:1, 0:P], bkv[:, :], start=True, stop=False)
                for k in range(K):
                    ins = mm(banks[6][0:P, :], xnT_s[:, u, k, :], wkv[:, k, :], start=False, stop=(k == K - 1))
                ins.then_inc(kv_done, 1)
                for k in range(K):
                    ins = mm(banks[u][0:P, 256:256 + R * H], xnT_s[:, u, k, :], wer[:, k, :],
                             start=(k == 0), stop=(k == K - 1))
                ins.then_inc(er_done, 1)

            def sum_kv(t, u, first=False, last=False):
                if not first:
                    pe.wait_ge(kv_scaled, t + 1)
                for hb in range(K):
                    ins = mm(banks[7][:, hb * 128:(hb + 1) * 128], kv_s[0:P, u, hb * 128:(hb + 1) * 128],
                             kv_s[0:P, u, D + hb * 128:D + (hb + 1) * 128],
                             start=first and hb == 0, stop=last, skip_group_check=True)
                ins.then_inc(kv_summed, 1)

            def window_pair_pe(i, last=False):
                for u in range(2):
                    t = 2 * i + u
                    window(t, u)
                    sum_kv(t - 1, 1 - u, first=isinstance(t, int) and t == 0)
                    if not last:
                        turn_window(t + 2, u)

            turn_window(0, 0)
            turn_window(1, 1)
            pe.wait_ge(weights_ready, 2)
            window_pair_pe(0)
            with pe.Fori(1, W // 2 - 1) as i:
                window_pair_pe(i)
            window_pair_pe(W // 2 - 1, last=True)
            sum_kv(W - 1, 1, last=True)

            pe.wait_ge(fold_ready, 1)
            pe.wait_ge(mixw_loaded, 16 * (2 + MH + 2 * K + FC + 1))
            for hb in range(K):
                mm(banks[0][:, hb * D:(hb + 1) * D], kvd[:, hb, :], wqT[:, hb, :], start=(hb == 0), stop=True,
                   skip_group_check=True)
                ins = mm(banks[1][:, hb:hb + 1], kvd[:, hb, :], bq[:, hb:hb + 1], start=(hb == 0), stop=True,
                         skip_group_check=True)
            ins.then_inc(fold_mm, 1)
            pe.wait_ge(fold_ready, 3)
            for k in range(K):
                for hb in range(K):
                    mm(banks[2][:, k * D:(k + 1) * D], mixT[:, hb, k * 128:(k + 1) * 128], w1m[:, hb, :],
                       start=(k == 0 and hb == 0), stop=True, skip_group_check=True)
            for k in range(K):
                for hb in range(K):
                    ins = mm(banks[3][:, k:k + 1], w1m[:, hb, k * 128:(k + 1) * 128], cvec[:, hb:hb + 1],
                             start=(k == 0 and hb == 0), stop=True, skip_group_check=True)
            ins.then_inc(fold_mm, 1)
            pe.wait_ge(fold_ready, 4)
            pe.wait_ge(xnT_kept, W)

            def mix_block_h(b, u):
                if not isinstance(b, int) or b >= 2:
                    pe.wait_ge(mix_gelu, (b - 1) * K)
                for k in range(K):
                    for q in range(K):
                        ins = mm(banks[u * K + k][:, 0:BN], weff[:, q, k * 128:(k + 1) * 128],
                                 xnT[:, q, bass.ds(b * BN, BN)], start=(q == 0), stop=(q == K - 1))
                    ins.then_inc(mix_h, 1)

            def mix_block_out(b, u):
                pe.wait_ge(mix_gelu, (b + 1) * K)
                for i in range(BLK):
                    t = b * BLK + i
                    if not isinstance(b, int) or t >= 2:
                        pe.wait_ge(mix_added, t - 1)
                    for k in range(K):
                        ins = mm(banks[4 + (u * BLK + i) % 2][0:P, 0:D], hT_m[u][:, k, i * P:(i + 1) * P], w2m[:, k, :],
                                 start=(k == 0), stop=(k == K - 1))
                    ins.then_inc(mix_out, 1)

            def mix_pair(i, last=False):
                mix_block_h(2 * i + 1, 1)
                mix_block_out(2 * i, 0)
                if not last:
                    mix_block_h(2 * i + 2, 0)
                mix_block_out(2 * i + 1, 1)

            mix_block_h(0, 0)
            mix_pair(0)
            with pe.Fori(1, NB // 2 - 1) as i:
                mix_pair(i)
            mix_pair(NB // 2 - 1, last=True)

            pe.wait_ge(masks_ready, 1)
            pe.wait_ge(mix_added, W)
            pe.sem_inc(er_further, 1)
            pe.sem_inc(sum_further, 1)

            def sum_er(c, n, u):
                v = u % 2
                wait(pe, carried, 2 * (c - 1))
                pe.wait_ge(pens_staged, c + 1)
                for q in range(2):
                    ins = turn(banks[2 + v][0:4, (2 + q) * P:(3 + q) * P], pens_now[0:P, u, q, :], ident[0:P, 0:P])
                ins.then_inc(pens_turned, 1)
                lo, up = span(pe, c)
                wait(pe, scores_done, c - 1)
                pe.wait_ge(dhot_first, c + 1)
                for j in range(J):
                    ins = mm(banks[v][0:P, j * R * H:(j + 1) * R * H], dhot[0][0:P, j * P:(j + 1) * P],
                             er_sb[0:P, bass.ds(lo * (R * H), R * H)], start=(j == 0), stop=True, skip_group_check=True)
                ins.then_inc(er_first, 1)

                def er_of(w):
                    pe.wait_ge(dhot_further, w)
                    for j in range(J):
                        ins = mm(banks[v][0:P, j * R * H:(j + 1) * R * H], dhot[1][0:P, j * P:(j + 1) * P],
                                 er_sb[0:P, bass.ds(w * (R * H), R * H)], start=False, stop=True, skip_group_check=True)
                    ins.then_inc(er_further, 1)

                further(pe, lo, up, er_of)

            def turn_tails(c, n, u):
                v = u % 2
                pe.wait_ge(runs_ready, c + 1)
                pe.wait_ge(pens_copied, c + 1)
                turn(banks[2 + v][0:4, 0:P], runF[0:P, v, :, J - 1], ident[0:P, 0:P])
                turn(banks[2 + v][0:4, P:2 * P], runB[0:P, v, :, 0], ident[0:P, 0:P]).then_inc(tails_turned, 1)

            def turn_carry(c, n, u):
                v = u % 2
                pe.wait_ge(carried, 2 * (c + 1))
                wait(pe, diff_ready, c - 1)
                wait(pe, acc_rescaled, c - 1)
                settle(pe)
                turn(banks[4 + v][0:P, 0:H], gx[:, v, 0:P], ident[0:4, 0:4])
                turn(banks[4 + v][0:P, H:2 * H], hx[:, v, 1:P + 1], ident[0:4, 0:4]).then_inc(carry_back, 1)

            def spread_fac(c, n, u):
                pe.wait_ge(facdiag_ready, c + 1)
                pe.wait_ge(diff_ready, c + 1)
                mm(banks[4 + u % 2][:, 2 * H:3 * H], ones[0:4, :], facdiag[:, :], start=True, stop=True,
                   skip_group_check=True).then_inc(fac_spread, 1)

            def place_sums(c, u):
                lo, up = span(pe, c)
                pe.wait_ge(ehot_first, c + 1)
                pe.wait_ge(scaled_vector, c + 1)
                pe.wait_ge(scaled_scalar, (J - JV) * H * (c + 1))
                wait(pe, kept_first, c)
                for j in range(J):
                    mm(banks[6][0:P, 0:ROW], ehot[0][0:P, j, :], ring[0:P, u, j, :], start=(j == 0), stop=False)
                pe.wait_ge(acc_rescaled, c + 1)
                mm(banks[6][0:P, 0:ROW], ident[0:P, 0:P], acc[0:P, bass.ds(lo, 1), :].rearrange("p w c -> p (w c)"),
                   start=False, stop=True).then_inc(sum_first, 1)

                def sum_of(w):
                    pe.wait_ge(ehot_further, w)
                    pe.wait_ge(kept_further, w)
                    for j in range(J):
                        ins = mm(banks[7][0:P, 0:ROW], ehot[1][0:P, j, :], ring[0:P, u, j, :],
                                 start=(j == 0), stop=(j == J - 1))
                    ins.then_inc(sum_further, 1)

                further(pe, lo, up, sum_of)

            def chunk_pe(c, n, u):
                turn_tails(c, n, u)
                if not isinstance(c, int) or c < NC - 1:
                    sum_er(c + 1, n, (u + 1) % U)
                turn_carry(c, n, u)
                if not isinstance(c, int) or c >= 1:
                    place_sums(c - 1, (u - 1) % U)
                spread_fac(c, n, u)

            sum_er(0, 0, 0)
            chunks(pe, chunk_pe)
            place_sums(NC - 1, (NC - 1) % U)

            def turn_y(b, u):
                for i in range(BLK):
                    t = b * BLK + i
                    pe.wait_ge(y_ready, t + 1)
                    if not isinstance(b, int) or b >= 2:
                        pe.wait_ge(yT_ready, t - 2 * BLK + 1)
                    for k in range(K):
                        ins = turn(banks[u * BLK + i][:, k * P:(k + 1) * P], xn_t[0:P, i, k * 128:(k + 1) * 128],
                                   ident[0:P, 0:P])
                    ins.then_inc(y_turned, 1)

            def gates(b, u):
                pe.wait_ge(yT_ready, (b + 1) * BLK)
                if not isinstance(b, int) or b >= 2:
                    pe.wait_ge(gate_out, 2 * (b - 1))
                for k in range(K):
                    ins = mm(banks[6 + u][0:1, 0:BN], wr[:, k:k + 1], xnT[:, k, bass.ds(b * BN, BN)],
                             start=(k == 0), stop=(k == K - 1))
                ins.then_inc(gate_row, 1)
                pe.wait_ge(gate_kept, b + 1)
                mm(banks[6 + u][:, 0:BN], ones[0:1, :], wst[:, u, :], start=True, stop=True, skip_group_check=True)
                for i in range(BLK):
                    ins = mm(banks[6 + u][0:P, BN + i:BN + i + 1], wst[:, u, i * P:(i + 1) * P], ones[0:1, 0:1],
                             start=False, stop=True, skip_group_check=True)
                ins.then_inc(gate_spread, 1)

            for u in range(2):
                turn_y(u, u)
                gates(u, u)
            with pe.Fori(1, NB // 2) as i:
                for u in range(2):
                    turn_y(2 * i + u, u)
                    gates(2 * i + u, u)

            pe.wait_ge(ffnw_loaded, 32)

            def ffn_hidden(b, u):
                for f in range(FC):
                    if not isinstance(b, int) or b * FC + f >= 4:
                        pe.wait_ge(ffn_gelu, b * FC + f - 3)
                    for k in range(K):
                        ins = mm(banks[f % 4][:, 0:BN], w1f[:, k, f * 128:(f + 1) * 128],
                                 xnT[:, k, bass.ds(b * BN, BN)], start=(k == 0), stop=(k == K - 1))
                    ins.then_inc(ffn_h, 1)

            def ffn_out(b, u):
                pe.wait_ge(ffn_gelu, (b + 1) * FC)
                for i in range(BLK):
                    t = b * BLK + i
                    if not isinstance(b, int) or t >= 2:
                        pe.wait_ge(ffn_z_out, t - 1)
                    for f in range(FC):
                        ins = mm(banks[4 + (u * BLK + i) % 2][0:P, 0:D], hT_f[u][:, f, i * P:(i + 1) * P], w2f[:, f, :],
                                 start=(f == 0), stop=(f == FC - 1))
                    ins.then_inc(ffn_z, 1)

            ffn_pairs(pe, ffn_hidden, ffn_out)

        @block.vector
        def _(dve):
            v_ = nc.vector
            own = Steps(dve, vector_step, settle)

            own(v_.memset(headmask[:, :], 0.0))
            for q in range(128 // MD):
                ins = v_.memset(headmask[q * MD:(q + 1) * MD, q * MD:(q + 1) * MD], 1.0 / N)
            own(ins)

            for g in range(3):
                dve.wait_ge(x_loaded[g], 32)
                if g == 0:
                    dve.wait_ge(consts_ready, 2)
                with dve.Fori(5 * g, 5 * g + 5) as i:
                    own.at(2 + 3 * i)
                    for u in range(2):
                        ins = v_.bn_stats(stats[0:P, u, :], x_sb[0:P, bass.ds(2 * i + u, 1), :].rearrange("p w d -> p (w d)"))
                    own(ins)
                    for u in range(2):
                        ins = v_.bn_aggr(mv2[0:P, u, :], stats[0:P, u, :])
                    own(ins)
                    own(v_.tensor_copy(mv[0:P, bass.ds(2 * i, 2), :], mv2[0:P, 0:2, :]))
            own.at(2 + 3 * W // 2)
            dve.sem_inc(var_ready, 1)

            dve.wait_ge(qkv_loaded, 32)
            heads = wqkv.rearrange("p k (h s d) -> p k h s d", s=3, d=MD)
            v_.tensor_copy(q_packed.rearrange("p k (h d) -> p k h d", d=MD), heads[:, :, :, 0, :]).then_inc(weights_ready, 1)
            for k in range(K):
                ins = v_.tensor_reduce(var16[:, k, :].rearrange("p (h s) -> p h s", s=2), heads[:, k, :, 1:3, :], AX.X, ALU.add)
            own(ins)
            for k in range(K):
                for i in range(2):
                    ins = v_.scalar_tensor_tensor(
                        wkv[:, k, i * D:(i + 1) * D].rearrange("p (h d) -> p h d", d=MD),
                        var16[:, k, :].rearrange("p (h s) -> p h s", s=2)[:, :, i].unsqueeze(2).to_broadcast([128, MH, MD]),
                        -1.0 / MD, heads[:, k, :, 1 + i, :], ALU.mult, ALU.add)
            own(ins)
            bheads = brow.rearrange("p (h s d) -> p h s d", s=3, d=MD)
            own(v_.tensor_reduce(var16[0:1, 0, :].rearrange("p (h s) -> p h s", s=2), bheads[:, :, 1:3, :], AX.X, ALU.add))
            for i in range(2):
                ins = v_.scalar_tensor_tensor(
                    bkv[:, i * D:(i + 1) * D].rearrange("p (h d) -> p h d", d=MD),
                    var16[0:1, 0, :].rearrange("p (h s) -> p h s", s=2)[:, :, i].unsqueeze(2).to_broadcast([1, MH, MD]),
                    -1.0 / MD, bheads[:, :, 1 + i, :], ALU.mult, ALU.add)
            own(ins)

            dve.wait_ge(conv_loaded, 16 * K)
            dve.wait_ge(attn_loaded, 32)
            for k in range(K):
                cols = waug[:, k, :, :].rearrange("p r (h c) -> p (r h) c", c=HC)
                for i, to in enumerate((cols[:, :, HD], wer[:, k, :])):
                    own(v_.tensor_tensor(attn_prod, cols[:, :, 0:HD], attn_b[i], ALU.mult))
                    own(v_.tensor_reduce(to, attn_prod, AX.X, ALU.add))
            dve.sem_inc(weights_ready, 1)

            dve.wait_ge(idx_loaded, 32)
            v_.scalar_tensor_tensor(row_idx[0:P], src_t[0:P], float(R), typ_t[0:P], ALU.mult, ALU.add).then_inc(idx_ready, 1)
            dve.wait_ge(edges_loaded, 48)
            own(v_.tensor_copy(dstf[0:P], dst10[0:P]))
            own(v_.tensor_copy(dfirstf[0:P, :], dfirst[0:P, :]))
            own(v_.tensor_copy(dlastf[:, :], dlast[:, :]))
            dve.wait_ge(std_ready, 1)
            own(v_.reciprocal(rstd[0:P, :], rstd[0:P, :]))

            def normalise(t, u):
                if not isinstance(t, int) or t >= 2:
                    dve.wait_ge(xn_turned, t - 1)
                    dve.wait_ge(xn_added, t - 1)
                v_.tensor_scalar(xn_t[0:P, u, :], x_sb[0:P, bass.ds(t, 1), :].rearrange("p w d -> p (w d)"),
                                 mv[0:P, bass.ds(t, 1), 0:1].rearrange("p w o -> p (w o)"), rstd[0:P, bass.ds(t, 1)],
                                 ALU.subtract, ALU.mult).then_inc(xn_ready, 1)

            def window_pair_dve(i, last=False):
                for u in range(2):
                    t = 2 * i + u
                    wait(dve, table_written[u], 32 * i)
                    for q in range(2):
                        dve.wait_ge(feat_odd_done, 2 * t + q + 1)
                        v_.tensor_copy(stage[u][0:P, 4 * q + 2:4 * q + 4, :], feat_ps[1][0:P]).then_inc(feat_odd_out, 1)
                    if not last:
                        normalise(t + 2, u)
                    dve.wait_ge(sq_ready, t + 1)
                    v_.tensor_reduce(var16[0:P, 0, :], sq[0:P].rearrange("p (q d) -> p q d", d=MD), AX.X, ALU.add)\
                      .then_inc(kvar_ready, 1)
                    dve.wait_ge(kstd_ready, t + 1)
                    v_.reciprocal(var16[0:P, 1, :], var16[0:P, 1, :]).then_inc(krstd_ready, 1)
                    dve.wait_ge(krstd_ready, t + 1)
                    wait(dve, kv_summed, t)
                    v_.tensor_tensor(kv_s[0:P, u, :].rearrange("p (q d) -> p q d", d=MD),
                                     banks[6][0:P, :].rearrange("p (q d) -> p q d", d=MD),
                                     var16[0:P, 1, :].unsqueeze(2).to_broadcast([P, 2 * MH, MD]), ALU.mult)\
                      .then_inc(kv_normed, 1)
                    dve.wait_ge(er_done, t + 1)
                    v_.tensor_copy(er_sb[0:P, bass.ds(t * (R * H), R * H)], banks[u][0:P, 256:256 + R * H]).then_inc(er_out, 1)

            def prepare_edges():
                own(v_.tensor_tensor(pen[0:P], dstf[0:P, :, 1:J + 2], dstf[0:P, :, 0:J + 1], ALU.is_equal))
                v_.memset(penF[0:P], NEG)
                v_.memset(penB[0:P], NEG)
                own(v_.tensor_scalar(pen[0:P], pen[0:P], -1.0, -NEG, ALU.add, ALU.mult))
                v_.tensor_copy(penF[0:P, :, :, 1:J], pen[0:P, :, 1:J].unsqueeze(2).to_broadcast([P, NC, H, J - 1]))
                for j in range(1, J):
                    v_.tensor_copy(penB[0:P, :, :, j], pen[0:P, :, J - j].unsqueeze(2).to_broadcast([P, NC, H]))
                v_.tensor_copy(penA[0:P, :, 0], pen[0:P, :, 0])
                own(v_.tensor_copy(penZ[0:P, :, J - 1], pen[0:P, :, J]))
                for j in range(1, J):
                    v_.tensor_tensor(penA[0:P, :, j], penA[0:P, :, j - 1], pen[0:P, :, j], ALU.min)
                    own(v_.tensor_tensor(penZ[0:P, :, J - 1 - j], penZ[0:P, :, J - j], pen[0:P, :, J - j], ALU.min))
                v_.tensor_copy(pen0[0:P], penA[0:P, :, J - 1].unsqueeze(2).to_broadcast([P, NC, H]))
                own(v_.tensor_copy(pen1[0:P], penZ[0:P, :, 0].unsqueeze(2).to_broadcast([P, NC, H])))
                own(v_.tensor_tensor(rel_hot[0:P].rearrange("p c j r -> p (c j) r"),
                                     typ_t[0:P].rearrange("p c j -> p (c j)").unsqueeze(2).to_broadcast([P, NC * J, R]),
                                     iota[0:P, 0:R].unsqueeze(1).to_broadcast([P, NC * J, R]), ALU.is_equal))
                own(v_.tensor_tensor(hi_cmp, dlastf[:, :].unsqueeze(2).to_broadcast([1, NC, W]),
                                     wbase[0:1, :].unsqueeze(1).to_broadcast([1, NC, W]), ALU.is_ge))
                own(v_.tensor_reduce(hi_f[:, 1:NC + 1], hi_cmp, AX.X, ALU.add))
                own(v_.tensor_scalar(hi_f[:, 1:NC + 1], hi_f[:, 1:NC + 1], -1.0, None, ALU.add))
                v_.memset(hi_f[:, 0:1], 0.0)
                own(v_.memset(hi_f[:, NC:NC + 1], float(W - 1)))
                v_.tensor_copy(hi[:, :], hi_f[:, :])
                own(v_.memset(acc[0:P, 0, :], 0.0))
                dve.sem_inc(masks_ready, 1)

            for u in range(2):
                normalise(u, u)
            window_pair_dve(0)
            prepare_edges()
            with dve.Fori(1, W // 2 - 1) as i:
                window_pair_dve(i)
            window_pair_dve(W // 2 - 1, last=True)

            dve.wait_ge(kv_summed, W + 1)
            v_.tensor_tensor(kvd, banks[7][:, 0:D].rearrange("p (k n) -> p k n", k=K),
                             headmask[:, :].unsqueeze(1).to_broadcast([128, K, 128]), ALU.mult).then_inc(fold_ready, 1)
            dve.wait_ge(fold_mm, 1)
            own(v_.tensor_copy(mixT, banks[0].rearrange("p (k n) -> p k n", k=K)))
            v_.tensor_copy(cvec, banks[1][:, 0:K]).then_inc(fold_ready, 1)
            for hb in range(K):
                diag = mixT[:, hb, hb * 128:(hb + 1) * 128]
                ins = v_.tensor_tensor(diag, diag, ident[:, :], ALU.add)
            ins.then_inc(fold_ready, 1)
            dve.wait_ge(fold_mm, 2)
            v_.tensor_copy(weff, banks[2].rearrange("p (k n) -> p k n", k=K))
            v_.tensor_tensor(beff[:, :], banks[3][:, 0:K], b1m[:, :], ALU.add).then_inc(fold_ready, 1)

            def mix_add(b, u):
                for i in range(BLK):
                    t = b * BLK + i
                    dve.wait_ge(mix_out, t + 1)
                    rows = x_sb[0:P, bass.ds(t, 1), :].rearrange("p w d -> p (w d)")
                    v_.tensor_tensor(rows, rows, banks[4 + (u * BLK + i) % 2][0:P, 0:D], ALU.add).then_inc(mix_added, 1)

            dve.wait_ge(xn_added, W)
            with dve.Fori(0, NB // 2) as i:
                for u in range(2):
                    mix_add(2 * i + u, u)

            def spread_dst(c, n, u):
                lo, up = span(dve, c)
                edges = dst_row[u % 2][0:P].rearrange("n (p j) -> n j p", j=J)
                dve.wait_ge(dst_row_loaded[u % 2], 16 * (n * (U // 2) + u // 2 + 1))
                wait(dve, er_first, c)
                v_.tensor_scalar(dhot[0][0:P].rearrange("n (j p) -> n j p", j=J), edges, nodecol[0:P, bass.ds(lo, 1)], None,
                                 ALU.is_equal).then_inc(dhot_first, 1)

                def spread_window(w):
                    dve.wait_ge(er_further, w)
                    v_.tensor_scalar(dhot[1][0:P].rearrange("n (j p) -> n j p", j=J), edges, nodecol[0:P, bass.ds(w, 1)],
                                     None, ALU.is_equal).then_inc(dhot_further, 1)

                further(dve, lo, up, spread_window)

            score_own = Steps(dve, score_step)
            carry_own = Steps(dve, carry_step)
            weight_own = Steps(dve, weight_step)
            place_own = Steps(dve, place_step)
            place_further_own = Steps(dve, place_further_step)

            def now(of, c):
                part = of[0:P, bass.ds(c, 1)]
                return part.rearrange("p c h j -> p (c h) j") if len(part.shape) == 4 else part.rearrange("p c j -> p (c j)")

            def scores(c, n, u):
                v = u % 2
                score_own.at(3 * c)
                up = dve.value_load(hi[0:1, bass.ds(c + 1, 1)], min_val=0, max_val=W - 1)
                dve.wait_ge(er_first, c + 1)
                dve.wait_ge(er_further, up + 1)
                v_.tensor_tensor(ersel[0:P], banks[v][0:P, 0:J * R * H].rearrange("p (j r h) -> p j h r", j=J, r=R),
                                 now(rel_hot, c).unsqueeze(2).to_broadcast([P, J, H, R]), ALU.mult).then_inc(scores_done, 1)
                dve.wait_ge(scores_done, c + 1)
                score_own(v_.tensor_reduce(er_e[0:P], ersel[0:P], AX.X, ALU.add))
                dve.wait_ge(gathered[u], 16 * J * (n + 1))
                el = ring[0:P, u].rearrange("p j (h c) -> p h j c", c=HC)[:, :, :, HD]
                score_own(v_.tensor_tensor(score[0:P], er_e[0:P].rearrange("p j h -> p h j"), el, ALU.add))
                v_.memset(ring[0:P, u].rearrange("p j (h c) -> p (j h) c", c=HC)[:, :, HD:HC], 1.0)
                score_own(v_.scalar_tensor_tensor(e_cur[0:P, v], score[0:P], 0.2, score[0:P], ALU.mult, ALU.max))
                e = e_cur[0:P, v].rearrange("p h j -> p (h j)")
                v_.tensor_tensor_scan(runF[0:P, v].rearrange("p h j -> p (h j)"), now(penF, c).rearrange("p h j -> p (h j)"),
                                      e, NEG, ALU.add, ALU.max)
                ins = v_.tensor_tensor_scan(reverse(runB[0:P, v].rearrange("p h j -> p (h j)")),
                                            now(penB, c).rearrange("p h j -> p (h j)"), reverse(e),
                                            NEG, ALU.add, ALU.max)
                ins.then_inc(runs_ready, 1)

            def carry(c, n, u):
                v = u % 2
                carry_own.at(c)
                dve.wait_ge(tails_turned, c + 1)
                dve.wait_ge(pens_copied, c + 1)
                tails = banks[2 + v][0:4]
                v_.tensor_copy(gx[:, v, 0:1], gx[:, 1 - v, P:P + 1])
                v_.tensor_tensor_scan(gx[:, v, 1:P + 1], penT[:, v, 0:P], tails[:, 0:P], gx[:, 1 - v, P:P + 1],
                                      ALU.add, ALU.max).then_inc(carried, 1)
                v_.tensor_tensor_scan(reverse(hx[:, v, 0:P]), reverse(penT[:, v, P:2 * P]), reverse(tails[:, P:2 * P]), NEG,
                                      ALU.add, ALU.max).then_inc(carried, 1)
                dve.wait_ge(carried, 2 * (c + 1))
                carry_own(v_.tensor_tensor(fac[:, 0:1], gx[:, v, 0:1], hx[:, v, 0:1], ALU.max))
                v_.tensor_tensor(fac[:, 1:2], gx[:, v, 0:1], fac[:, 0:1], ALU.subtract).then_inc(fac_diff, 1)

            def spread_factors(c):
                dve.wait_ge(fac_exp, c + 1)
                wait(dve, fac_spread, c)
                v_.scalar_tensor_tensor(facdiag[:, :], ident[0:4, 0:4], fac[:, 2:3], ident[0:4, 0:4], ALU.mult, ALU.subtract)\
                  .then_inc(facdiag_ready, 1)

            def weights(c, n, u):
                v = u % 2
                weight_own.at(3 * c)
                dve.wait_ge(carry_back, c + 1)
                back = banks[4 + v][0:P]
                for q, p in enumerate((penA, penZ)):
                    v_.tensor_tensor(cmx[0:P, q], back[:, q * H:(q + 1) * H].unsqueeze(2).to_broadcast([P, H, J]),
                                     now(p, c).unsqueeze(1).to_broadcast([P, H, J]), ALU.add)
                weight_own(v_.tensor_tensor(cmx[0:P, 2], runF[0:P, v], runB[0:P, v], ALU.max))
                weight_own(v_.tensor_tensor(cmx[0:P, 0], cmx[0:P, 0], cmx[0:P, 1], ALU.max))
                weight_own(v_.tensor_tensor(cmx[0:P, 0], cmx[0:P, 0], cmx[0:P, 2], ALU.max))
                v_.tensor_tensor(diff[0:P, v], e_cur[0:P, v], cmx[0:P, 0], ALU.subtract).then_inc(diff_ready, 1)

            def scale(c, n, u):
                dve.wait_ge(ex_ready, c + 1)
                part = ring[0:P, u, 0:JV].rearrange("p j (h c) -> p j h c", c=HC)
                v_.tensor_tensor(part, part, ex[0:P, u, :, 0:JV].rearrange("p h j -> p j h").unsqueeze(3)
                                 .to_broadcast([P, JV, H, HC]), ALU.mult).then_inc(scaled_vector, 1)

            def place(c, u):
                lo, up = span(dve, c)
                place_own.at(3 * c)
                runs = now(dstf, c)[:, 1:J + 1]
                place_own(v_.tensor_scalar(dloc[0:P, 0, :], runs, wbase[0:P, bass.ds(lo, 1)], None, ALU.subtract))
                wait(dve, sum_first, c)
                v_.tensor_tensor(ehot[0][0:P], iota[0:P, :].unsqueeze(1).to_broadcast([P, J, P]),
                                 dloc[0:P, 0, :].unsqueeze(2).to_broadcast([P, J, P]), ALU.is_equal).then_inc(ehot_first, 1)
                dve.wait_ge(fac_spread, c + 1)
                place_own(v_.tensor_scalar(eqc[0:P, :], dfirstf[0:P, bass.ds(c, 1)], nodecol[0:P, bass.ds(lo, 1)], None,
                                           ALU.is_equal))
                place_own(v_.tensor_scalar(fsc[0:P, :], banks[4 + u % 2][0:P, 2 * H:3 * H], eqc[0:P, :], 1.0, ALU.mult, ALU.add))
                wait(dve, kept_first, c)
                dve.wait_ge(kept_further, lo + 1)
                rows = acc[0:P, bass.ds(lo, 1), :].rearrange("p w (h c) -> p (w h) c", c=HC)
                v_.tensor_tensor(rows, rows, fsc[0:P, :].unsqueeze(2).to_broadcast([P, H, HC]), ALU.mult)\
                  .then_inc(acc_rescaled, 1)

                def place_window(w):
                    place_further_own.at(w - 1)
                    place_further_own(v_.tensor_scalar(dloc[0:P, 1, :], runs, wbase[0:P, bass.ds(w, 1)], None, ALU.subtract))
                    dve.wait_ge(sum_further, w)
                    v_.tensor_tensor(ehot[1][0:P], iota[0:P, :].unsqueeze(1).to_broadcast([P, J, P]),
                                     dloc[0:P, 1, :].unsqueeze(2).to_broadcast([P, J, P]), ALU.is_equal)\
                      .then_inc(ehot_further, 1)

                further(dve, lo, up, place_window)

            def chunk_dve(c, n, u):
                scores(c, n, u)
                if not isinstance(c, int) or c < NC - 1:
                    spread_dst(c + 1, n + (u + 1) // U, (u + 1) % U)
                carry(c, n, u)
                if not isinstance(c, int) or c >= 1:
                    place(c - 1, (u - 1) % U)
                spread_factors(c)
                weights(c, n, u)
                scale(c, n, u)

            v_.memset(gx[:, 1, P:P + 1], NEG)
            own(v_.memset(hx[:, :, P:P + 1], NEG))
            spread_dst(0, 0, 0)
            chunks(dve, chunk_dve)
            place(NC - 1, (NC - 1) % U)

            dve.wait_ge(kept_first, NC)
            dve.wait_ge(kept_further, W)
            heads_of = flat_acc[0:P, :].rearrange("p (q c) -> p q c", c=HC)
            rden_q = rden[0:P].rearrange("p w h -> p (w h)")
            x2_own = Steps(dve, x2_step, settle)
            x2_own(v_.tensor_scalar(rden_q, heads_of[:, :, HD], 1e-30, None, ALU.max))
            x2_own(v_.reciprocal(rden_q, rden_q))
            with dve.Fori(0, NB) as b:
                x2_own.at(2 + 5 * b)
                sums = acc[0:P, bass.ds(b * BLK, BLK), :].rearrange("p w (h c) -> p (w h) c", c=HC)[:, :, 0:HD]
                x2_own(v_.tensor_tensor(sums, sums, rden[0:P, bass.ds(b * BLK, BLK), :].rearrange("p w h -> p (w h)")
                                        .unsqueeze(2).to_broadcast([P, BLK * H, HD]), ALU.mult))
                rows = x_sb[0:P, bass.ds(b * BLK, BLK), :].rearrange("p w (h d) -> p (w h) d", d=HD)
                x2_own(v_.tensor_tensor(rows, rows, sums, ALU.add))
                for i in range(BLK):
                    ins = v_.bn_stats(stats[0:P, i, :], x_sb[0:P, bass.ds(b * BLK + i, 1), :].rearrange("p w d -> p (w d)"))
                x2_own(ins)
                for i in range(BLK):
                    ins = v_.bn_aggr(mv2[0:P, i, :], stats[0:P, i, :])
                x2_own(ins)
                x2_own(v_.tensor_copy(mv[0:P, bass.ds(b * BLK, BLK), :], mv2[0:P, 0:BLK, :]))
            dve.sem_inc(x2_var, 1)
            dve.wait_ge(x2_std, 1)
            x2_own.at(2 + 5 * NB)
            x2_own(v_.reciprocal(rstd[0:P, :], rstd[0:P, :]))

            def norm_y(b, u):
                for i in range(BLK):
                    t = b * BLK + i
                    if not isinstance(b, int) or b >= 1:
                        dve.wait_ge(y_turned, t - BLK + 1)
                        dve.wait_ge(y_added, t - BLK + 1)
                    v_.tensor_scalar(xn_t[0:P, i, :], x_sb[0:P, bass.ds(t, 1), :].rearrange("p w d -> p (w d)"),
                                     mv[0:P, bass.ds(t, 1), 0:1].rearrange("p w o -> p (w o)"), rstd[0:P, bass.ds(t, 1)],
                                     ALU.subtract, ALU.mult).then_inc(y_ready, 1)

            def keep_gates(b, u):
                dve.wait_ge(gate_spread, b + 1)
                v_.tensor_copy(wall[:, bass.ds(b * BN, BN)], banks[6 + u][:, 0:BN]).then_inc(gate_out, 1)
                v_.tensor_copy(wcol[0:P, bass.ds(b * BLK, BLK)], banks[6 + u][0:P, BN:BN + BLK]).then_inc(gate_out, 1)

            norm_y(0, 0)
            norm_y(1, 1)
            keep_gates(0, 0)
            with dve.Fori(1, NB // 2) as i:
                norm_y(2 * i, 0)
                keep_gates(2 * i - 1, 1)
                norm_y(2 * i + 1, 1)
                keep_gates(2 * i, 0)
            keep_gates(NB - 1, 1)
            dve.wait_ge(gate_out, 2 * NB)

            top = Steps(dve, topk_step)
            top(v_.tensor_scalar(picked[:, :], pcol[:, :], 1, None, ALU.max))
            for r, (shift, _) in enumerate(ROUNDS):
                v_.tensor_scalar(psh[:, r:r + 1], pcol[:, :] if r else picked[:, :], shift, None, ALU.logical_shift_left)
            v_.memset(prefix[:, :], 0)
            v_.tensor_scalar(pmask[:, 0:1], pcolf[:, :], 1.0, None, ALU.is_ge)
            top(v_.tensor_scalar(pmask[:, 1:2], pcolf[:, :], 64.0, None, ALU.is_lt))
            top(v_.tensor_tensor(pmask[:, 1:2], pmask[:, 1:2], pmask[:, 0:1], ALU.mult))

            def as_float(key):
                top(v_.tensor_scalar(cand[:, 1:2], key, 31, -1, ALU.arith_shift_right, ALU.bitwise_xor))
                top(v_.tensor_scalar(cand[:, 1:2], cand[:, 1:2], -2 ** 31, None, ALU.bitwise_or))
                top(v_.tensor_tensor(cand[:, 2:3], key, cand[:, 1:2], ALU.bitwise_xor))
                return cand[:, 2:3].bitcast(F32)

            for r, (shift, six) in enumerate(ROUNDS):
                top(v_.tensor_tensor(cand[:, 0:1], prefix[:, :], psh[:, r:r + 1], ALU.bitwise_or))
                at_least = as_float(cand[:, 0:1])
                top(v_.tensor_scalar(count_out, wall, at_least, 0.0, ALU.is_ge, ALU.add, accum_out=count[:, 2:3]))
                v_.scalar_tensor_tensor(count[:, 0:1], count[:, 2:3], float(TOPK), pmask[:, six:six + 1], ALU.is_ge, ALU.mult)\
                  .then_inc(flag_ready, 1)
                dve.wait_ge(flag_summed, r + 1)
                top(v_.tensor_copy(picked[:, :], count[:, 1:2]))
                top(v_.tensor_scalar(picked[:, :], picked[:, :], shift, None, ALU.logical_shift_left))
                top(v_.tensor_tensor(prefix[:, :], prefix[:, :], picked[:, :], ALU.bitwise_or))
            limit = as_float(prefix[:, :])
            top(v_.tensor_scalar(count_out, wall, limit, 0.0, ALU.is_gt, ALU.add, accum_out=count[:, 2:3]))
            v_.tensor_scalar(count[:, 3:4], count[:, 2:3], -1.0, float(TOPK), ALU.mult, ALU.add)
            top(v_.tensor_scalar(at_limit, wall, limit, None, ALU.is_equal))
            top(v_.tensor_tensor_scan(at_limit, ones[:, 0:1].to_broadcast([128, N]), at_limit, 0.0, ALU.mult, ALU.add))
            top(v_.tensor_scalar(count_out, at_limit, count[:, 3:4], 0.0, ALU.is_le, ALU.add, accum_out=count[:, 2:3]))
            v_.tensor_scalar(tie[0:P, 0, :], wcol[0:P, :], limit[0:P], None, ALU.is_equal)
            v_.tensor_scalar(tie[0:P, 1, :], nodecol[0:P, :], count[0:P, 2:3], None, ALU.is_lt)
            top(v_.tensor_scalar(wsel[0:P, :], wcol[0:P, :], limit[0:P], None, ALU.is_gt))
            top(v_.tensor_tensor(tie[0:P, 0, :], tie[0:P, 0, :], tie[0:P, 1, :], ALU.mult))
            top(v_.tensor_tensor(wsel[0:P, :], wsel[0:P, :], tie[0:P, 0, :], ALU.add))
            top(v_.tensor_tensor(wsel[0:P, :], wsel[0:P, :], wcol[0:P, :], ALU.mult))

            dve.wait_ge(y_added, W)
            with dve.Fori(0, W) as t:
                dve.wait_ge(ffn_z_bias, t + 1)
                rows = acc[0:P, bass.ds(t, 1), 0:D].rearrange("p w d -> p (w d)")
                v_.scalar_tensor_tensor(rows, rows, wsel[0:P, bass.ds(t, 1)],
                                        x_sb[0:P, bass.ds(t, 1), :].rearrange("p w d -> p (w d)"), ALU.mult, ALU.add)\
                  .then_inc(rows_done, 1)


_INS = ("x", "src", "dst", "edge_type_8", "L0_gnn_conv_weights", "L0_gnn_attn_l", "L0_gnn_attn_r", "L0_gnn_h_bias",
        "L0_mix_w_qkv", "L0_mix_b_qkv", "L0_mix_kln_g", "L0_mix_kln_b", "L0_mix_vln_g", "L0_mix_vln_b", "L0_mix_w1",
        "L0_mix_b1", "L0_mix_w2", "L0_mix_b2", "L0_ffn_wr", "L0_ffn_br", "L0_ffn_w1", "L0_ffn_b1", "L0_ffn_w2",
        "L0_ffn_b2")


def kernel(**inputs):
    import concourse.bacc as bacc
    import numpy as np
    from concourse.bass_utils import run_bass_kernel_spmd

    nc = bacc.Bacc("TRN2", target_bir_lowering=False, num_devices=1)
    arrays = {name: np.ascontiguousarray(inputs[name]) for name in _INS}
    handles = {name: nc.dram_tensor(name, array.shape, mybir.dt.from_np(array.dtype), kind="ExternalInput").ap()
               for name, array in arrays.items()}
    out = nc.dram_tensor("out", (N, D), F32, kind="ExternalOutput").ap()
    graph_layer(nc, handles, out)
    result = run_bass_kernel_spmd(nc, [arrays], core_ids=[0])
    return result.results[0]["out"]
```

```python
from contextlib import ExitStack

import concourse.bass as bass
from concourse import mybir

F32 = mybir.dt.float32
F32R = mybir.dt.float32r
BF16 = mybir.dt.bfloat16
I32 = mybir.dt.int32
ALU = mybir.AluOpType
ACT = mybir.ActivationFunctionType
AX = mybir.AxisListType
SUM = bass.bass_isa.ReduceOp.add

N, D = 3750, 256
P = 125
W = N // P
K = D // 128
R, H, HD = 8, 4, 64
HC = HD + 1
ROW = H * HC
E = 60000
J = 8
CH = P * J
NC = E // CH
PIECES = 3
U = 10
RING = 4
LAG = 4
JV = 4
MH, MD = 8, 32
F = 4 * D
FC = F // 128
BLK = 3
NB = W // BLK
BN = BLK * P
BNE = BN + BN % 2
AHEAD = 4
TOPK = N // 2 - 1
EPS = 1e-5
NEG = -1e30
PARTS = ((0, 112), (112, P))
DIGIT = 4
CANDS = 1 << DIGIT
ROUNDS = 32 // DIGIT


def wait(eng, signal, value):
    if not isinstance(value, int) or value > 0:
        eng.wait_ge(signal, value)


class Steps:

    def __init__(self, eng, counter, settle=None):
        self.eng, self.counter, self.base, self.k, self.settle = eng, counter, 0, 0, settle

    def at(self, base):
        self.base, self.k = base, 0

    def __call__(self, ins):
        self.k += 1
        ins.then_inc(self.counter, 1)
        self.eng.wait_ge(self.counter, self.base + self.k)
        if self.settle and not isinstance(self.base, int):
            self.settle(self.eng)


def reverse(ap):
    part, (step, n) = ap.ap
    return bass.AP(ap.tensor, ap.offset + step * (n - 1), [part, (-step, n)])


def graph_layer(nc, a, out):
    with ExitStack() as ctx:
        def sb(name, shape, dt=F32):
            return ctx.enter_context(nc.sbuf_tensor(name, shape, dt))

        def next_at():
            return -(-nc.sbuf_base // 32) * 32

        def sb_at(name, shape, dt, at):
            return nc.alloc_sbuf_tensor_at(name, shape, dt, offset=at)

        def sem(name):
            return ctx.enter_context(nc.semaphore(name))

        table = nc.dram_tensor("feature_table", (N * R, ROW), F32).ap()
        dst_ends = nc.dram_tensor("dst_of_chunks", (2, NC), I32).ap()
        attended = nc.dram_tensor("attended", (N + P, ROW), F32).ap()
        er_table = nc.dram_tensor("dst_scores", (N + P, PIECES * R * H), BF16).ap()
        dst_pad = nc.dram_tensor("dst_padded", (1, E + 2), I32).ap()
        sort_key = nc.dram_tensor("sort_key", (1, E), F32).ap()
        sorted_src, sorted_typ = (nc.dram_tensor(name, (1, E + 2), I32).ap() for name in ("sorted_src", "sorted_typ"))

        x_sb = sb("x_sb", [128, W, D])
        xnT_at = next_at()
        xnT = sb("xnT", [128, K, N])
        acc_at = next_at()
        acc = sb("acc", [128, W, ROW])
        ring_at = next_at()
        ring = sb("ring", [128, RING, J, ROW])
        waug_at = next_at()
        waug = sb("waug", [128, K, R, ROW])
        arena_at = next_at()
        arena = sb("arena", [128, 6000])
        w_hi = sb_at("w_hi", [128, K, R, ROW], F32R, ring_at + 2 * J * ROW * 4)
        w_lo = sb_at("w_lo", [128, K, R, ROW], F32R, waug_at)
        wkv_hi = sb_at("wkv_hi", [128, K, 2 * D], F32R, arena_at)
        wkv_lo = sb_at("wkv_lo", [128, K, 2 * D], F32R, arena_at + 1536 * 4)
        xn_lo = sb_at("xn_lo", [128, 2, K, P], F32R, arena_at + 1024 * 4)
        xn_hi = sb_at("xn_hi", [128, 2, K, P], F32R, arena_at + 4608 * 4)
        ones_r = sb_at("ones_r", [1, 128], F32R, arena_at + 5120 * 4)
        bkv_hi = sb_at("bkv_hi", [1, 2 * D], F32R, acc_at + 1144 * 4)
        masks_at = next_at()
        masks = sb("masks", [128, 7680], BF16)
        y_hi = sb_at("y_hi", [128, 2, K, BNE], F32R, arena_at + FC * BN * 4)
        y_lo = sb_at("y_lo", [128, 2, K, BNE], F32R, xnT_at + (2 * K * BNE + K * F + FC * D) * 4)
        h_hi = [sb_at(f"h_hi{u}", [128, FC, BN], F32R, at) for u, at in enumerate((arena_at, masks_at))]
        h_lo = sb_at("h_lo", [128, 2, FC, BN], F32R, ring_at)
        ffnw_hi = sb_at("ffnw_hi", [128, K * F + FC * D], F32R, xnT_at + 2 * K * BNE * 4)
        ffnw_lo = sb_at("ffnw_lo", [128, K * F + FC * D], F32R, waug_at)
        wer = sb("wer", [128, K, R * H])
        w1m = sb("w1m", [128, K, D])
        w2m = sb("w2m", [128, K, D])
        bkv_at = next_at()
        bkv = sb("bkv", [1, 2 * D])
        bkv_lo = sb_at("bkv_lo", [1, 2 * D], F32R, bkv_at)
        bq = sb("bq", [128, K])
        b1m = sb("b1m", [128, K])
        beff = sb("beff", [128, K])
        b1f = sb("b1f", [128, FC])
        br = sb("br", [128, 1])
        bias_rows = sb("bias_rows", [128, 3, D])
        ident = sb("ident", [128, 128])
        headmask = sb("headmask", [128, 128])
        ones = sb("ones", [128, 128])
        upto = sb("upto", [128, 128])
        iota = sb("iota", [128, P])
        wbase = sb("wbase", [128, W])
        stats = sb("stats", [128, AHEAD, 6])
        mv2 = sb("mv2", [128, AHEAD, 2])
        mv = sb("mv", [128, W, 2])
        rstd = sb("rstd", [128, W])
        epsc = sb("epsc", [128, 1])
        var16 = sb("var16", [128, 2, 2 * MH])
        xn_t = sb("xn_t", [128, BLK, D])
        xnT_s = sb("xnT_s", [128, 2, K, P])
        er_row = sb("er_row", [128, 3, R * H])
        er_out_row = sb("er_out_row", [128, 2, PIECES, R * H], BF16)
        er_now = sb("er_now", [128, 2, PIECES, R * H], BF16)
        er_far = sb("er_far", [128, PIECES, R * H], BF16)
        row_idx = sb("row_idx", [128, NC, J], I32)
        idx_now = sb("idx_now", [128, U, J], I32)
        penAZ = sb("penAZ", [128, NC, 2, J], BF16)
        penA = penAZ[:, :, 0, :]
        penZ = penAZ[:, :, 1, :]
        pen0 = sb("pen0", [128, NC, H])
        pen1 = sb("pen1", [128, NC, H])
        first_node = sb("first_node", [1, NC], I32)
        descents = sb("descents", [128, 1])
        descents_row = sb("descents_row", [1, P])
        unsorted_f = sb("unsorted_f", [1, 1])
        unsorted = sb("unsorted", [1, 1], I32)
        edge_now = sb("edge_now", [128, 4, J], I32)
        hi = sb("hi", [1, NC + 4], I32)
        sentinel = sb("sentinel", [1, 1], I32)
        fac = sb("fac", [4, 3])
        facdiag = sb("facdiag", [4, 4])
        dloc = sb("dloc", [128, NC, J])
        node = sb("node", [128, NC])
        rowhot = sb("rowhot", [128, NC])
        pens_now = sb("pens_now", [128, U, 2, H])
        pcolf = sb("pcolf", [128, 1])
        digit = sb("digit", [128, CANDS - 1], I32)
        prefix = sb("prefix", [128, 1], I32)
        cand = sb("cand", [128, 3, CANDS - 1], I32)
        count = sb("count", [128, CANDS - 1])
        total = sb("total", [128, CANDS - 1])
        reached = sb("reached", [128, CANDS - 1])
        found = sb("found", [128, 1])
        foundi = sb("foundi", [128, 1], I32)
        left = sb("left", [128, 2])

        banks = []
        for i in range(4):
            pair = ctx.enter_context(nc.psum_tensor(f"bank{2 * i}", [128, 2, 512], F32))
            banks += [pair[:, 0, :], pair[:, 1, :]]
            if i == 1:
                feat_ps = [pair[:, :, 0:ROW]]
            if i == 2:
                feat_ps.append(pair[:, :, 0:ROW])

        flat_acc = acc[:, :, :].rearrange("p w c -> p (w c)")
        sq = flat_acc[:, 6144:6144 + 2 * D]
        typ_t = flat_acc[:, 6660:7140].bitcast(I32).rearrange("p (c j) -> p c j", j=J)
        src_t = flat_acc[:, 7140:7620].bitcast(I32).rearrange("p (c j) -> p c j", j=J)
        ends = flat_acc[:, 7620:7620 + 2 * NC].bitcast(I32)
        endsf = flat_acc[:, 4600:4600 + 2 * NC]
        spread = flat_acc[:, 4800:4800 + NC]
        lastrow = flat_acc[:, 4900:4900 + NC + 1]
        same = flat_acc[:, 5000:5000 + NC + 1]
        summed = [flat_acc[:, 4000 + i * ROW:4000 + (i + 1) * ROW] for i in range(2)]
        acc_slots = [flat_acc[:, lo:lo + J * ROW].rearrange("p (j c) -> p j c", c=ROW) for lo in (0, 4000 + 2 * ROW)]
        hi_f = flat_acc[:, 3600:3600 + NC + 4]
        dstf = flat_acc[:, 5100:5100 + NC * (J + 2)].rearrange("p (c j) -> p c j", j=J + 2)
        pen = flat_acc[:, 0:NC * (J + 1)].rearrange("p (c j) -> p c j", j=J + 1)
        hi_cmp = flat_acc[:, 1660:1660 + NC * W].rearrange("p (c w) -> p c w", w=W)
        dst10 = flat_acc[:, 540:540 + NC * (J + 2)].bitcast(I32).rearrange("p (c j) -> p c j", j=J + 2)
        stage = [ring[:, u, :, :] for u in range(2)]
        flat_ring = ring[:, :, :, :].rearrange("p u j c -> p (u j c)")
        attn_b = [xnT[:, i, 2 * P:2 * P + R * D].rearrange("p (q d) -> p q d", d=HD) for i in range(2)]
        src_prod = flat_ring[:, 0:R * D].rearrange("p (q d) -> p q d", d=HD)
        dst_prod = [masks[:, 0:2 * R * D].bitcast(F32), flat_acc[:, 1900:1900 + R * D]]
        dst_prod = [part.rearrange("p (q d) -> p q d", d=HD) for part in dst_prod]
        hT_f = [flat_ring[:, i * FC * BN:(i + 1) * FC * BN].rearrange("p (f n) -> p f n", f=FC) for i in range(2)]
        flat_waug = waug[:, :, :, :].rearrange("p k r c -> p (k r c)")
        ffnw = flat_waug[:, 0:K * F + FC * D]
        w1f_parts, w2f_parts = ([part[:, lo:lo + n].rearrange("p (k f) -> p k f", k=k) for part in (ffnw_hi, ffnw_lo)]
                                for lo, n, k in ((0, K * F, K), (K * F, FC * D, FC)))
        w1f = flat_waug[:, 0:K * F].rearrange("p (k f) -> p k f", k=K)
        w2f = flat_waug[:, K * F:K * F + FC * D].rearrange("p (f n) -> p f n", f=FC)

        free0, free1 = xnT[:, 0, 2 * P:], xnT[:, 1, 2 * P:]
        key_row, place_row = free0[:, 0:CH], free0[:, CH:2 * CH]
        key, rank = (free1[:, i * NC * J:(i + 1) * NC * J].rearrange("p (c j) -> p c j", j=J) for i in range(2))
        descent = free1[:, 2 * NC * J:3 * NC * J].rearrange("p (c j) -> p c j", j=J)
        place_col = free1[:, 3 * NC * J:3 * NC * J + J]
        fewer = free1[:, 3 * NC * J + J:3 * NC * J + 2 * J]
        less = flat_acc[:, 1900:1900 + 2 * CH].rearrange("p (j e) -> p j e", j=2)

        flat_xnT = xnT[:, :, :].rearrange("p k n -> p (k n)")
        taken = [0]

        def scratch(*shape, parts=128):
            size = 1
            for n in shape:
                size *= n
            taken[0] += size
            part = flat_xnT[0:parts, taken[0] - size:taken[0]]
            names = "abc"[:len(shape)]
            return part.rearrange(f"p ({' '.join(names)}) -> p {' '.join(names)}", **dict(zip(names, shape)))

        dloc_further = scratch(1, J)
        node_further = scratch(1, 1)
        carry_sel = scratch(2, H)
        ersel = scratch(J, H, R)
        er_e = scratch(J, H)
        score = scratch(H, J)
        e_cur = scratch(2, H, J)
        cmx = [scratch(4, H, J) for _ in range(2)]
        runF = [m[:, 2] for m in cmx]
        runB = [m[:, 3] for m in cmx]
        peak = scratch(H, J)
        diff = scratch(2, H, J)
        ex = scratch(U, H, J)
        penT = scratch(2, 2 * P, parts=4)
        gx = scratch(2, P + 1, parts=4)
        hx = scratch(2, P + 1, parts=4)

        spare = flat_ring[:, 2 * FC * BN:]
        rdens = spare[:, 0:2 * BLK * H]
        wcol, wsel = (spare[:, (H + i) * W:(H + 1 + i) * W] for i in range(2))
        tie = spare[:, (H + 2) * W:(H + 6) * W].rearrange("p (i w) -> p i w", w=W)
        y_f = flat_xnT[:, 0:2 * K * BNE].rearrange("p (u k n) -> p u k n", u=2, k=K)
        waug_slots, xnT_slots = ([flat[:, lo:lo + J * ROW].rearrange("p (j c) -> p j c", c=ROW) for lo in (at, at + J * ROW)]
                                 for flat, at in ((flat_waug, 0), (flat_xnT, K * N - 2 * J * ROW)))
        slots = [ring[:, u] for u in range(RING)] + acc_slots + waug_slots + xnT_slots
        products = spare[:, 300:300 + BLK * D].rearrange("p (i d) -> p i d", d=D)
        compared = spare[:, 1100:1100 + (CANDS - 1) * W].rearrange("p (j w) -> p j w", w=W)

        def words(lo, n, k):
            return arena[:, lo:lo + n * k].rearrange("p (k n) -> p k n", k=k)

        wqkv = words(0, 3 * D, K)
        wkv = words(1536, 2 * D, K)
        gam = arena[:, 2560:3072]
        bet = arena[:, 3072:3584]
        kv_s = words(3584, 2 * D, 2)
        q_packed = words(3584, D, K)
        brow = arena[0:1, 4608:5376]
        wqT = words(5376, D, K)
        kvd = words(1536, 128, K)
        mixT = words(1792, D, K)
        cvec = arena[:, 2304:2304 + K]
        weff = words(2560, D, K)
        hT_m = [words(3072 + i * K * BN, BN, K) for i in range(2)]
        dst_row = [arena[:, i * CH:(i + 1) * CH].bitcast(I32) for i in range(2)]
        dhot = [arena[:, 2 * CH + i * CH // 2:2 * CH + (i + 1) * CH // 2].bitcast(BF16) for i in range(2)]
        ehot = [words((3 + i) * CH, P, J) for i in range(3)]
        rel_hot = masks[:, 0:3840].rearrange("p (c j r) -> p c j r", j=J, r=R)
        penF = masks[:, 3840:5760].rearrange("p (c h j) -> p c h j", h=H, j=J)
        penB = masks[:, 5760:7680].rearrange("p (c h j) -> p c h j", h=H, j=J)

        def dram(ap, offset, pattern):
            return bass.AP(ap.tensor, offset, pattern)

        x_loaded = [sem(f"x_loaded{g}") for g in range(3)]
        idents_ready = sem("idents_ready")
        descents_ready = sem("descents_ready")
        descents_loaded = sem("descents_loaded")
        unsorted_ready = sem("unsorted_ready")
        sort_step = sem("sort_step")
        keys_ready = sem("keys_ready")
        keys_written = sem("keys_written")
        key_row_loaded = sem("key_row_loaded")
        key_row_used = sem("key_row_used")
        places_ready = sem("places_ready")
        edge_staged = sem("edge_staged")
        edge_scattered = sem("edge_scattered")
        stat_step = sem("stat_step")
        inv_step = sem("inv_step")
        src_folded = sem("src_folded")
        xn_split = sem("xn_split")
        split_step = sem("split_step")
        ffnw_hi_ready = sem("ffnw_hi_ready")
        ffnw_split = sem("ffnw_split")
        hidden_split = sem("hidden_split")
        src_fold = sem("src_fold")
        w_hi_ready = sem("w_hi_ready")
        kv_centred = sem("kv_centred")
        kv_hi_ready = sem("kv_hi_ready")
        kv_split = sem("kv_split")
        dst_folded = sem("dst_folded")
        dst_products = sem("dst_products")
        dst_copied = sem("dst_copied")
        first_copied = sem("first_copied")
        edges_loaded = sem("edges_loaded")
        conv_loaded = [sem(f"conv_loaded{k}") for k in range(K)]
        attn_loaded = [sem(f"attn_loaded{i}") for i in range(2)]
        qkv_loaded = sem("qkv_loaded")
        mixw_loaded = sem("mixw_loaded")
        rows_loaded = sem("rows_loaded")
        ffnw_loaded = sem("ffnw_loaded")
        pool_step = sem("pool_step")
        consts_ready = sem("consts_ready")
        vector_step = sem("vector_step")
        var_ready = sem("var_ready")
        std_ready = sem("std_ready")
        weights_ready = sem("weights_ready")
        idx_ready = sem("idx_ready")
        xn_ready = sem("xn_ready")
        xn_turned = sem("xn_turned")
        xn_added = sem("xn_added")
        xnT_ready = sem("xnT_ready")
        xnT_kept = sem("xnT_kept")
        feat_done = sem("feat_done")
        feat_out = sem("feat_out")
        table_written = [sem(f"table_written{u}") for u in range(2)]
        kv_done = sem("kv_done")
        er_done = sem("er_done")
        er_out = sem("er_out")
        sq_ready = sem("sq_ready")
        kvar_ready = sem("kvar_ready")
        kstd_ready = sem("kstd_ready")
        krstd_ready = sem("krstd_ready")
        kv_normed = sem("kv_normed")
        kv_scaled = sem("kv_scaled")
        kv_summed = sem("kv_summed")
        wq_turned = sem("wq_turned")
        wqT_ready = sem("wqT_ready")
        fold_mm = sem("fold_mm")
        fold_ready = sem("fold_ready")
        masks_ready = sem("masks_ready")
        mix_h = sem("mix_h")
        mix_gelu = sem("mix_gelu")
        mix_out = sem("mix_out")
        mix_added = sem("mix_added")
        idx_staged = sem("idx_staged")
        gathered = [sem(f"gathered{u}") for u in range(U)]
        dst_row_loaded = [sem(f"dst_row_loaded{v}") for v in range(2)]
        dhot_first = sem("dhot_first")
        dhot_further = sem("dhot_further")
        er_first = sem("er_first")
        er_further = sem("er_further")
        score_step = sem("score_step")
        scores_done = sem("scores_done")
        pens_turned = sem("pens_turned")
        pens_copied = sem("pens_copied")
        pens_staged = sem("pens_staged")
        runs_ready = sem("runs_ready")
        tails_turned = sem("tails_turned")
        carried = sem("carried")
        carry_step = sem("carry_step")
        fac_diff = sem("fac_diff")
        fac_exp = sem("fac_exp")
        facdiag_ready = sem("facdiag_ready")
        fac_spread = sem("fac_spread")
        carry_back = sem("carry_back")
        weight_step = sem("weight_step")
        diff_ready = sem("diff_ready")
        ex_ready = sem("ex_ready")
        scaled_vector = sem("scaled_vector")
        scaled_scalar = sem("scaled_scalar")
        spread_step = sem("spread_step")
        place_further_step = sem("place_further_step")
        ehot_first = sem("ehot_first")
        ehot_further = sem("ehot_further")
        carry_ready = sem("carry_ready")
        er_far_loaded = sem("er_far_loaded")
        er_now_loaded = [sem(f"er_now_loaded{v}") for v in range(2)]
        er_step = sem("er_step")
        er_split = sem("er_split")
        er_written = [sem(f"er_written{u}") for u in range(2)]
        zeros_ready = sem("zeros_ready")
        zeroed = sem("zeroed")
        sums_written = sem("sums_written")
        sums_loaded = [sem(f"sums_loaded{g}") for g in range(2)]
        wr_loaded = sem("wr_loaded")
        sum_first = sem("sum_first")
        sum_further = sem("sum_further")
        kept_first = sem("kept_first")
        kept_further = sem("kept_further")
        x2_step = sem("x2_step")
        x2_var = sem("x2_var")
        x2_std = sem("x2_std")
        norm_step = sem("norm_step")
        gated = sem("gated")
        y_ready = sem("y_ready")
        y_turned = sem("y_turned")
        y_added = sem("y_added")
        yT_ready = sem("yT_ready")
        ffn_h = sem("ffn_h")
        ffn_gelu = sem("ffn_gelu")
        ffn_z = sem("ffn_z")
        ffn_z_out = sem("ffn_z_out")
        ffn_z_bias = sem("ffn_z_bias")
        topk_step = sem("topk_step")
        counted = sem("counted")
        totalled = sem("totalled")
        tie_ready = sem("tie_ready")
        tie_ranked = sem("tie_ranked")
        rows_done = sem("rows_done")
        settled = sem("settled")
        out_written = sem("out_written")

        block = ctx.enter_context(nc.Block())

        def settle(eng):
            eng.sem_inc(settled, 1)

        def chunks(eng, body, windows=False):
            known = []

            def load(c):
                return eng.value_load(hi[0:1, bass.ds(c, 1)], min_val=0, max_val=W - 1)

            def chunk(c, n, u):
                if not windows:
                    return body(c, n, u)
                later = []
                body(c, n, u, known[-5:], lambda: later.append(load(c + 3)))
                known.extend(later)

            if windows:
                known += [None, None, load(0), load(1), load(2)]
            for u in range(U):
                chunk(u, 0, u)
            kept = [eng.alloc_register(f"window{k}_{eng.engine.name}") for k in range(5)] if windows else []
            for reg, value in zip(kept, known[-5:]):
                eng.reg_mov(reg, value)
            with eng.Fori(1, NC // U - 1) as n:
                known = [eng.snap(reg, min_val=0, max_val=W - 1) for reg in kept]
                for u in range(U):
                    chunk(n * U + u, n, u)
                for reg, value in zip(kept, known[-5:]):
                    eng.reg_mov(reg, value)
            known = [eng.snap(reg, min_val=0, max_val=W - 1) for reg in kept]
            for u in range(U):
                chunk(NC - U + u, NC // U - 1, u)
            return known[-5:]

        def second_half(eng, norm, hidden, rows, between=None):
            norm(0, 0)
            hidden(0, 0)
            norm(1, 1)

            def pair(i, last=False):
                hidden(2 * i + 1, 1)
                if not last:
                    norm(2 * i + 2, 0)
                rows(2 * i, 0)
                if last and between:
                    between()
                if not last:
                    norm(2 * i + 3, 1)
                    hidden(2 * i + 2, 0)
                rows(2 * i + 1, 1)

            pair(0)
            with eng.Fori(1, NB // 2 - 2) as i:
                pair(i)
            pair(NB // 2 - 2)
            pair(NB // 2 - 1, last=True)

        def within(eng, reg, value, most):
            eng.reg_mov(reg, value)
            return eng.snap(reg, min_val=0, max_val=most)

        def further(eng, lo, up, body):
            with eng.If(lo < up):
                with eng.Fori(lo + 1, up + 1) as w:
                    body(w)

        @block.sync
        def _(sp):
            sp.dma_start(dram(dst_pad, 1, [[N, 16], [1, N]]), dram(a["dst"], 0, [[N, 16], [1, N]])).then_inc(dst_copied, 16)
            sp.wait_ge(consts_ready, 1)
            for at in (0, E + 1):
                sp.dma_start(dst_pad[0:1, at:at + 1], sentinel[:, :]).then_inc(dst_copied, 16)
            sp.wait_ge(conv_loaded[1], 16)
            sp.wait_ge(dst_copied, 48)

            def load_edges(src, typ, at, again=0):
                sp.dma_start(dst10[0:P], dram(dst_pad, 0, [[J, P], [CH, NC], [1, J + 2]])).then_inc(edges_loaded, 16)
                for i, end in enumerate((1, CH)):
                    sp.dma_start(dst_ends[i:i + 1, :], dram(dst_pad, end, [[0, 1], [CH, NC]]), allow_slow_non_contiguous=True)\
                      .then_inc(first_copied, 16)
                for ap, to in ((src, src_t), (typ, typ_t)):
                    sp.dma_start(to[0:P], dram(ap, at, [[J, P], [CH, NC], [1, J]])).then_inc(edges_loaded, 16)
                sp.wait_ge(first_copied, 32 * (again + 1))
                sp.dma_start(ends[0:P], dram(dst_ends, 0, [[0, P], [1, 2 * NC]])).then_inc(edges_loaded, 16)

            for to, gain, lo in ((gam, "L0_mix_kln_g", 0), (gam, "L0_mix_vln_g", D),
                                 (bet, "L0_mix_kln_b", 0), (bet, "L0_mix_vln_b", D)):
                sp.dma_start(to[:, lo:lo + D].rearrange("p (h d) -> p h d", d=MD),
                              dram(a[gain], 0, [[0, 128], [0, MH], [1, MD]])).then_inc(rows_loaded, 16)
            for i, name in enumerate(("L0_gnn_h_bias", "L0_mix_b2", "L0_ffn_b2")):
                sp.dma_start(bias_rows[:, i, :], dram(a[name], 0, [[0, 128], [1, D]])).then_inc(rows_loaded, 16)
            load_edges(a["src"], a["edge_type_8"], 0)

            sp.dma_start(w1m[:, :, :], a["L0_mix_w1"].rearrange("(k p) n -> p k n", p=128)).then_inc(mixw_loaded, 16)
            sp.dma_start(w2m[:, :, :], a["L0_mix_w2"].rearrange("(k p) n -> p k n", p=128)).then_inc(mixw_loaded, 16)
            for h in range(MH):
                sp.dma_start(bq[h % 4 * MD:(h % 4 + 1) * MD, h // 4:h // 4 + 1],
                             dram(a["L0_mix_b_qkv"], h * 3 * MD, [[1, MD], [1, 1]])).then_inc(mixw_loaded, 16)
            for to, name, n in ((b1m, "L0_mix_b1", K), (b1f, "L0_ffn_b1", FC)):
                for k in range(n):
                    sp.dma_start(to[:, k:k + 1], dram(a[name], k * 128, [[1, 128], [1, 1]])).then_inc(mixw_loaded, 16)

            sp.wait_ge(descents_ready, 1)
            sp.dma_start(descents_row[:, :], descents[0:P, :], allow_slow_non_contiguous=True).then_inc(descents_loaded, 16)
            sp.wait_ge(unsorted_ready, 1)
            settle(sp)
            with sp.If(sp.value_load(unsorted[0:1, 0:1], min_val=0, max_val=1) > 0):
                sp.wait_ge(keys_ready, 1)
                sp.dma_start(dram(sort_key, 0, [[J, P], [CH, NC], [1, J]]), key[0:P]).then_inc(keys_written, 16)
                sp.wait_ge(keys_written, 16)
                with sp.Fori(0, NC) as piece:
                    sp.wait_ge(key_row_used, piece + 1)
                    settle(sp)
                    sp.dma_start(key_row, dram(sort_key, piece * CH, [[0, 128], [1, CH]])).then_inc(key_row_loaded, 16)
                sp.wait_ge(edge_scattered, 16 * 3 * J * NC)
                load_edges(sorted_src, sorted_typ, 1, again=1)

            sp.wait_ge(zeros_ready, 1)
            sp.dma_start(attended.rearrange("(p i) c -> p i c", p=P),
                         summed[0][0:P].unsqueeze(1).to_broadcast([P, (N + P) // P, ROW])).then_inc(zeroed, 16)
            sp.dma_start(er_table[N:N + P, :], summed[0][0:P, 0:PIECES * R * H // 2].bitcast(BF16)).then_inc(zeroed, 16)

            def write_table(i):
                for u in range(2):
                    t = 2 * i + u
                    sp.wait_ge(feat_out, R // 2 * (t + 1))
                    for p0, p1 in PARTS:
                        sp.dma_start(
                            table[bass.ds(t * P * R + p0 * R, (p1 - p0) * R), :].rearrange("(p r) c -> p r c", r=R),
                            stage[u][p0:p1]).then_inc(table_written[u], 16)
                    sp.wait_ge(er_split, t + 1)
                    sp.dma_start(er_table[bass.ds(t * P, P), :], er_out_row[0:P, u].rearrange("p q r -> p (q r)"))\
                      .then_inc(er_written[u], 16)

            with sp.Fori(0, W // 2) as i:
                write_table(i)

            sp.wait_ge(consts_ready, 2)
            sp.dma_start(bias_rows[:, 1, :], dram(a["L0_ffn_wr"], 0, [[0, 128], [1, D]])).then_inc(wr_loaded, 16)
            sp.dma_start(br[:, :], dram(a["L0_ffn_br"], 0, [[0, 128], [1, 1]])).then_inc(wr_loaded, 16)

            sp.wait_ge(mix_added, W)
            sp.wait_ge(masks_ready, 1)
            sp.wait_ge(zeroed, 32)
            for u in range(2):
                sp.wait_ge(er_written[u], 16 * (W // 2))

            spare_sp = sp.alloc_register("spare_sp")

            def first_of(c):
                return sp.value_load(first_node[0:1, bass.ds(c, 1)], min_val=0, max_val=N - 1)

            def spans_of(c):
                return (sp.value_load(hi[0:1, bass.ds(c + i, 1)], min_val=0, max_val=W - 1) for i in range(2))

            def load_chunk(c, u):
                node0 = first_of(c)
                wait(sp, scores_done, c - 1)
                settle(sp)
                sp.dma_start(dst_row[u % 2], dram(dst_pad, c * CH + 1, [[0, 128], [1, CH]]))\
                  .then_inc(dst_row_loaded[u % 2], 16)
                sp.dma_start(er_now[0:P, u % 2].rearrange("p q r -> p (q r)"), er_table[bass.ds(node0, P), :])\
                  .then_inc(er_now_loaded[u % 2], 16)

            def load_further(c):
                lo, up = spans_of(c)

                def load_span(w):
                    at = within(sp, spare_sp, first_of(c) + (w - lo) * P, N - 1)
                    sp.wait_ge(er_further, w)
                    settle(sp)
                    sp.dma_start(er_far[0:P].rearrange("p q r -> p (q r)"),
                                 er_table[bass.ds(at, P), :])\
                      .then_inc(er_far_loaded, 16)

                further(sp, lo, up, load_span)

            def store_first(c, u, lo):
                node0 = first_of(c)
                sp.wait_ge(kept_first, c + 1)
                if not isinstance(c, int) or c >= 1:
                    sp.wait_ge(sums_written, 16 * (c + lo))
                settle(sp)
                sp.dma_start(attended[bass.ds(node0, P), :], summed[u % 2][0:P]).then_inc(sums_written, 16)

            def store(c, u):
                lo, up = spans_of(c)
                with sp.If(lo >= up):
                    store_first(c, u, lo)

            def store_long(c, u):
                lo, up = spans_of(c)
                with sp.If(lo < up):
                    store_first(c, u, lo)
                    with sp.Fori(lo + 1, up + 1) as w:
                        at = within(sp, spare_sp, first_of(c) + (w - lo) * P, N - 1)
                        sp.wait_ge(kept_further, w + 1)
                        settle(sp)
                        sp.wait_ge(sums_written, 16 * (c + w))
                        settle(sp)
                        sp.dma_start(attended[bass.ds(at, P), :],
                                     summed[u % 2][0:P]).then_inc(sums_written, 16)

            def chunk_sp(c, n, u):
                load_chunk(c, u)
                if not isinstance(c, int) or c >= LAG:
                    store(c - LAG, u)
                if not isinstance(c, int) or c >= LAG - 1:
                    store_long(c - LAG + 1, (u + 1) % U)
                load_further(c)

            chunks(sp, chunk_sp)
            for u in range(LAG):
                store(NC - LAG + u, u)
                if u + 1 < LAG:
                    store_long(NC - LAG + u + 1, u + 1)

            all_further = sp.value_load(hi[0:1, NC:NC + 1], min_val=0, max_val=W - 1)
            sp.wait_ge(sums_written, 16 * (all_further + NC))
            for g, (w0, w1) in enumerate(((0, 2 * BLK), (2 * BLK, W))):
                if g == 1:
                    sp.dma_start(w1f, a["L0_ffn_w1"].rearrange("(k p) f -> p k f", p=128)).then_inc(ffnw_loaded, 16)
                    sp.dma_start(w2f, a["L0_ffn_w2"].rearrange("(f p) n -> p f n", p=128)).then_inc(ffnw_loaded, 16)
                for p0, p1 in PARTS:
                    sp.dma_start(acc[p0:p1, w0:w1, :],
                                 attended[0:N, :].rearrange("(w p) c -> p w c", p=P)[p0:p1, w0:w1, :])\
                      .then_inc(sums_loaded[g], 16)

            with sp.Fori(0, NB) as b:
                sp.wait_ge(rows_done, b * BLK + BLK)
                for p0, p1 in PARTS:
                    sp.dma_start(out[bass.ds(b * BN, BN), :].rearrange("(w p) d -> p w d", p=P)[p0:p1],
                                 acc[p0:p1, bass.ds(b * BLK, BLK), 0:D]).then_inc(out_written, 16)
            sp.wait_ge(out_written, 32 * NB)

        @block.gpsimd
        def _(pool):
            own = Steps(pool, pool_step, settle)
            g = nc.gpsimd
            g.memset(sentinel[:, :], -1).then_inc(consts_ready, 1)
            g.memset(kv_s[:, 1, :], 0.0)
            g.memset(epsc[:, :], EPS)
            g.memset(ones[:, :], 1.0)
            g.memset(ident[:, :], 0.0)
            g.memset(upto[:, :], 1.0)
            g.memset(count[:, :], 0.0)
            g.iota(digit[:, :], [[1, CANDS - 1]], base=1, channel_multiplier=0)
            g.iota(iota[:, :], [[1, P]], base=0, channel_multiplier=0, allow_small_or_imprecise_dtypes=True)
            g.iota(wbase[:, :], [[P, W]], base=0, channel_multiplier=0, allow_small_or_imprecise_dtypes=True)
            own(g.iota(pcolf[:, :], [[0, 1]], base=0, channel_multiplier=1, allow_small_or_imprecise_dtypes=True))
            own(g.affine_select(out=ident[:, :], in_=ident[:, :], compare_op=ALU.not_equal, fill=1.0,
                                base=0, pattern=[[-1, 128]], channel_multiplier=1))
            own(g.affine_select(out=upto[:, :], in_=upto[:, :], compare_op=ALU.is_ge, fill=0.0,
                                base=0, pattern=[[1, 128]], channel_multiplier=-1))
            g.sem_inc(idents_ready, 1)
            pool.wait_ge(attn_loaded[1], 16)
            for k in range(K):
                pool.wait_ge(conv_loaded[k], 16)
                g.tensor_tensor(dst_prod[k], waug[:, k, :, :].rearrange("p r (h c) -> p (r h) c", c=HC)[:, :, 0:HD],
                                attn_b[1], ALU.mult).then_inc(dst_products, 1)
            pool.wait_ge(rows_loaded, 16 * 7)
            g.tensor_tensor(bias_rows[0:P, 0, :], bias_rows[0:P, 0, :], bias_rows[0:P, 1, :], ALU.add)\
             .then_inc(consts_ready, 1)
            pool.wait_ge(consts_ready, 2)

            def add_xn(t, u):
                rows = x_sb[0:P, bass.ds(t, 1), :].rearrange("p w d -> p (w d)")
                pool.wait_ge(xn_ready, t + 1)
                settle(pool)
                own(g.tensor_tensor(rows, rows, xn_t[0:P, u, :], ALU.add))
                g.tensor_tensor(rows, rows, bias_rows[0:P, 0, :], ALU.add).then_inc(xn_added, 1)

            def window_pair(i, last=False):
                for u in range(2):
                    t = 2 * i + u
                    own.at(4 + 3 * t)
                    if not (last and u == 1):
                        add_xn(t + 1, 1 - u)
                    pool.wait_ge(xnT_ready, t + 1)
                    settle(pool)
                    g.tensor_copy(xnT[:, :, bass.ds(t * P, P)], xnT_s[:, u, :, :]).then_inc(xnT_kept, 1)
                    pool.wait_ge(kv_normed, t + 1)
                    own(g.tensor_tensor(kv_s[0:P, u, :], kv_s[0:P, u, :], gam[0:P, :], ALU.mult))
                    own(g.tensor_tensor(kv_s[0:P, u, :], kv_s[0:P, u, :], bet[0:P, :], ALU.add))
                    g.sem_inc(kv_scaled, 1)

            add_xn(0, 0)
            window_pair(0)
            pool.wait_ge(unsorted_ready, 1)
            settle(pool)
            with pool.If(pool.value_load(unsorted[0:1, 0:1], min_val=0, max_val=1) > 0):
                g.iota(place_row, [[1, CH]], base=0, channel_multiplier=0, allow_small_or_imprecise_dtypes=True)
                g.iota(place_col, [[1, J]], base=0, channel_multiplier=J, allow_small_or_imprecise_dtypes=True)\
                 .then_inc(places_ready, 1)
                with pool.Fori(0, NC) as c:
                    pool.wait_ge(edge_staged, c + 1)
                    settle(pool)
                    for j in range(J):
                        for q, to in enumerate((dst_pad, sorted_src, sorted_typ)):
                            g.indirect_dma_start(dram(to, 0, [[1, E + 2], [1, 1]]),
                                                 bass.IndirectOffsetOnAxis(ap=edge_now[0:P, 0, j:j + 1], axis=0),
                                                 edge_now[0:P, 1 + q, j:j + 1], None).then_inc(edge_scattered, 16)
            with pool.Fori(1, W // 2 - 1) as i:
                window_pair(i)
            window_pair(W // 2 - 1, last=True)

            for u in range(2):
                pool.wait_ge(table_written[u], 32 * (W // 2))

            def gather(c, n, u):
                if not isinstance(c, int) or c >= U:
                    pool.wait_ge(tails_turned, c - U + 3)
                if isinstance(c, int) and c == U - len(xnT_slots):
                    pool.wait_ge(mix_added, W)
                pool.wait_ge(idx_staged, c + 1)
                settle(pool)
                for j in range(J):
                    g.indirect_dma_start(slots[u][0:P, j, :], None, table,
                                         bass.IndirectOffsetOnAxis(ap=idx_now[0:P, u, j:j + 1], axis=0))\
                     .then_inc(gathered[u], 16)

            chunks(pool, gather)

            def add_y(b):
                for i in range(BLK):
                    t = b * BLK + i
                    pool.wait_ge(y_ready, t + 1)
                    settle(pool)
                    rows = x_sb[0:P, bass.ds(t, 1), :].rearrange("p w d -> p (w d)")
                    g.tensor_tensor(rows, rows, xn_t[0:P, i, :], ALU.add).then_inc(y_added, 1)

            with pool.Fori(0, NB) as b:
                add_y(b)

            with pool.Fori(0, ROUNDS + 1) as r:
                pool.wait_ge(counted, r + 1)
                settle(pool)
                g.partition_all_reduce(total[:, :], count[:, :], 128, SUM).then_inc(totalled, 1)

            with pool.Fori(0, W) as t:
                pool.wait_ge(ffn_z_out, t + 1)
                settle(pool)
                rows = acc[0:P, bass.ds(t, 1), 0:D].rearrange("p w d -> p (w d)")
                g.tensor_tensor(rows, rows, bias_rows[0:P, 2, :], ALU.add).then_inc(ffn_z_bias, 1)

        @block.scalar
        def _(act):
            s = nc.scalar
            def load_x(g, w0, w1):
                for p0, p1 in PARTS:
                    act.dma_start(x_sb[p0:p1, w0:w1, :], a["x"].rearrange("(w p) d -> p w d", p=P)[p0:p1, w0:w1, :])\
                       .then_inc(x_loaded[g], 16)

            def load_conv(k):
                act.dma_start(waug[:, k, :, :].rearrange("p r (h c) -> p (r h) c", c=HC)[:, :, 0:HD],
                              dram(a["L0_gnn_conv_weights"], k * 128 * HD, [[HD, 128], [D * HD, R * H], [1, HD]]))\
                   .then_inc(conv_loaded[k], 16)

            def load_attn(i, name):
                act.dma_start(attn_b[i].rearrange("p q d -> p (q d)"), dram(a[name], 0, [[0, 128], [1, R * D]]))\
                   .then_inc(attn_loaded[i], 16)

            load_x(0, 0, AHEAD)
            load_conv(0)
            load_attn(0, "L0_gnn_attn_l")
            load_attn(1, "L0_gnn_attn_r")
            act.dma_start(wqkv, a["L0_mix_w_qkv"].rearrange("(k p) n -> p k n", p=128)).then_inc(qkv_loaded, 16)
            act.dma_start(brow, dram(a["L0_mix_b_qkv"], 0, [[0, 1], [1, 3 * D]])).then_inc(qkv_loaded, 16)
            load_conv(1)
            load_x(1, AHEAD, W // 2)
            load_x(2, W // 2, W)

            def row_std(k, t, n):
                act.wait_ge(var_ready, k)
                s.activation(rstd[0:P, bass.ds(t, n)], mv[0:P, bass.ds(t, n), 1], ACT.Sqrt, bias=epsc[0:P, :]).then_inc(std_ready, 1)

            act.wait_ge(idents_ready, 1)
            row_std(1, 0, AHEAD)
            def turned(t, u):
                act.wait_ge(xn_turned, t + 1)
                if not isinstance(t, int) or t >= 2:
                    act.wait_ge(kv_done, t - 1)
                    act.wait_ge(xnT_kept, t - 1)
                s.activation(xnT_s[:, u, :, :], banks[u][:, 0:K * P].rearrange("p (k n) -> p k n", k=K),
                             ACT.Copy).then_inc(xnT_ready, 1)

            def keep_features(t, u):
                for q in range(R // 2):
                    act.wait_ge(feat_done, R // 2 * t + q + 1)
                    s.activation(stage[u][0:P, 2 * q:2 * q + 2, :], feat_ps[q % 2][0:P], ACT.Copy).then_inc(feat_out, 1)

            def window_pair_act(i, last=False, stats=True):
                for u in range(2):
                    t = 2 * i + u
                    wait(act, table_written[u], 32 * i)
                    keep_features(t, u)
                    act.wait_ge(kv_done, t + 1)
                    wait(act, kvar_ready, t)
                    s.activation(sq[0:P], banks[6][0:P, :], ACT.Square).then_inc(sq_ready, 1)
                    act.wait_ge(kvar_ready, t + 1)
                    s.activation(var16[0:P, 1, :], var16[0:P, 0, :], ACT.Sqrt, bias=epsc[0:P, :], scale=1.0 / MD)\
                     .then_inc(kstd_ready, 1)
                    if not last:
                        turned(t + 2, u)
                    if stats and u == 0:
                        row_std(i + 2, 2 * i + AHEAD, 2)

            turned(0, 0)
            turned(1, 1)
            act.wait_ge(qkv_loaded, 32)
            s.activation(q_packed.rearrange("p k (h d) -> p k h d", d=MD),
                         wqkv.rearrange("p k (h s d) -> p k h s d", s=3, d=MD)[:, :, :, 0, :], ACT.Copy).then_inc(weights_ready, 1)
            act.wait_ge(src_fold, 1)
            s.activation(w_hi[:, 0], waug[:, 0], ACT.Copy).then_inc(w_hi_ready, 1)
            act.wait_ge(kv_centred, 1)
            act.wait_ge(weights_ready, 1)
            s.activation(wkv_hi[:, :, :], wkv, ACT.Copy)
            s.activation(bkv_hi[:, :], bkv[:, :], ACT.Copy).then_inc(kv_hi_ready, 1)
            act.wait_ge(wq_turned, 1)
            s.activation(wqT, banks[7].rearrange("p (k n) -> p k n", k=K), ACT.Copy).then_inc(wqT_ready, 1)
            act.wait_ge(src_fold, 2)
            s.activation(w_hi[:, 1], waug[:, 1], ACT.Copy).then_inc(w_hi_ready, 1)
            window_pair_act(0)
            with act.Fori(1, W // 2 - 2) as i:
                window_pair_act(i)
            window_pair_act(W // 2 - 2, stats=False)
            window_pair_act(W // 2 - 1, last=True, stats=False)

            def stage_chunk(c, u):
                s.activation(idx_now[0:P, u, :], row_idx[0:P, bass.ds(c, 1), :].rearrange("p c j -> p (c j)"), ACT.Copy)\
                 .then_inc(idx_staged, 1)
                for q, p in enumerate((pen0, pen1)):
                    ins = s.activation(pens_now[0:P, u, q, :], p[0:P, bass.ds(c, 1), :].rearrange("p c h -> p (c h)"), ACT.Copy)
                ins.then_inc(pens_staged, 1)

            act.wait_ge(idx_ready, 1)
            act.wait_ge(masks_ready, 1)
            for c in range(U - 1):
                stage_chunk(c, c)

            act.wait_ge(fold_ready, 4)

            def mix_hidden(b, u):
                for k in range(K):
                    act.wait_ge(mix_h, b * K + k + 1)
                    if k == 0 and (not isinstance(b, int) or b >= 2):
                        act.wait_ge(mix_out, (b - 1) * BLK)
                    s.activation(hT_m[u][:, k, :], banks[u * K + k][:, 0:BN], ACT.Gelu, bias=beff[:, k:k + 1])\
                     .then_inc(mix_gelu, 1)

            for u in range(2):
                mix_hidden(u, u)
            with act.Fori(1, NB // 2) as i:
                for u in range(2):
                    mix_hidden(2 * i + u, u)

            act.sem_inc(kept_further, 1)
            act.wait_ge(zeroed, 32)

            def copy_pens(c, n, u):
                act.wait_ge(pens_turned, c + 1)
                wait(act, carried, 2 * (c - 1))
                s.activation(penT[:, u % 2, :], banks[2 + u % 2][0:4, 2 * P:4 * P], ACT.Copy).then_inc(pens_copied, 1)

            def keep_first(c, u, lo):
                act.wait_ge(sum_first, c + 1)
                if not isinstance(c, int) or c >= 2:
                    act.wait_ge(sums_written, 16 * (c - 1 + lo))
                s.activation(summed[u % 2][0:P], banks[6 + u % 2][0:P, 0:ROW], ACT.Copy).then_inc(kept_first, 1)

            def keep(c, u, lo, up):
                with act.If(lo >= up):
                    keep_first(c, u, lo)

            def keep_long(c, u, lo, up):
                with act.If(lo < up):
                    keep_first(c, u, lo)
                    with act.Fori(lo + 1, up + 1) as w:
                        act.wait_ge(sum_further, w + 1)
                        act.wait_ge(sums_written, 16 * (c + w))
                        s.activation(summed[u % 2][0:P], banks[1][0:P, 0:ROW], ACT.Copy).then_inc(kept_further, 1)

            def edge_weights(c, u):
                act.wait_ge(diff_ready, c + 1)
                if not isinstance(c, int) or c >= U:
                    act.wait_ge(scaled_vector, c - U + 1)
                s.activation(ex[0:P, u], diff[0:P, u % 2], ACT.Exp).then_inc(ex_ready, 1)
                act.wait_ge(ex_ready, c + 1)
                for j in range(JV, J):
                    for h in range(H):
                        part = slots[u][0:P, j, h * HC:(h + 1) * HC]
                        s.activation(part, part, ACT.Copy, scale=ex[0:P, u, h, j:j + 1]).then_inc(scaled_scalar, 1)

            def chunk_act(c, n, u, win, load_next):
                copy_pens(c, n, u)
                if not isinstance(c, int) or c >= 1:
                    edge_weights(c - 1, (u - 1) % U)
                act.wait_ge(fac_diff, c + 1)
                s.activation(fac[:, 2:3], fac[:, 1:2], ACT.Exp).then_inc(fac_exp, 1)
                load_next()
                if not isinstance(c, int) or c < NC - U + 1:
                    stage_chunk(c + U - 1, (u + U - 1) % U)
                if not isinstance(c, int) or c >= 2:
                    keep(c - 2, u, win[0], win[1])
                if not isinstance(c, int) or c >= 1:
                    keep_long(c - 1, (u - 1) % U, win[1], win[2])

            win = chunks(act, chunk_act, windows=True)
            edge_weights(NC - 1, (NC - 1) % U)
            keep(NC - 2, (NC - 2) % U, win[0], win[1])
            keep(NC - 1, (NC - 1) % U, win[1], win[2])
            keep_long(NC - 1, (NC - 1) % U, win[1], win[2])

            def std(b, u):
                act.wait_ge(x2_var, b + 1)
                s.activation(rstd[0:P, u * BLK:(u + 1) * BLK], mv[0:P, u * BLK:(u + 1) * BLK, 1], ACT.Sqrt,
                             bias=epsc[0:P, :]).then_inc(x2_std, 1)

            def keep_turned(b, u):
                for i in range(BLK):
                    t = b * BLK + i
                    act.wait_ge(y_turned, t + 1)
                    if i == 0 and (not isinstance(b, int) or b >= 2):
                        act.wait_ge(ffn_h, (b - 1) * FC)
                    s.activation(y_f[:, u, :, i * P:(i + 1) * P],
                                 banks[6 + (u * BLK + i) % 2][:, 0:K * P].rearrange("p (k n) -> p k n", k=K), ACT.Copy)\
                     .then_inc(yT_ready, 1)
                if not isinstance(b, int) or b < NB - 1:
                    std(b + 1, 1 - u)

            def ffn_gelus(b, u):
                for f in range(FC):
                    act.wait_ge(ffn_h, b * FC + f + 1)
                    if f == 0 and (not isinstance(b, int) or b >= 2):
                        act.wait_ge(ffn_z, (b - 1) * BLK)
                    for to in (hT_f[u][:, f, :], h_hi[u][:, f, :]):
                        ins = s.activation(to, banks[f % 4][:, 0:BN], ACT.Gelu_apprx_tanh, bias=b1f[:, f:f + 1])
                    ins.then_inc(ffn_gelu, 1)

            def ffn_rows(b, u):
                for i in range(BLK):
                    t = b * BLK + i
                    act.wait_ge(ffn_z, t + 1)
                    s.activation(acc[0:P, bass.ds(t, 1), 0:D].rearrange("p w d -> p (w d)"),
                                 banks[4 + (u * BLK + i) % 2][0:P, 0:D], ACT.Copy).then_inc(ffn_z_out, 1)

            std(0, 0)
            act.wait_ge(ffnw_loaded, 32)
            for at in (0, K * F):
                s.activation(ffnw_hi[:, at:at + K * F], ffnw[:, at:at + K * F], ACT.Copy).then_inc(ffnw_hi_ready, 1)
            second_half(act, keep_turned, ffn_gelus, ffn_rows)

        @block.tensor
        def _(pe):
            mm = nc.tensor.matmul

            def mm_parts(to, x_hi, x_lo, w_hi, w_lo, first, last):
                for i, (x, w) in enumerate(((x_hi, w_hi), (x_hi, w_lo), (x_lo, w_hi))):
                    ins = mm(to, x, w, start=first and i == 0, stop=last and i == 2)
                return ins

            turn = nc.tensor.transpose

            def turn_window(t, u):
                pe.wait_ge(xn_ready, t + 1)
                if not isinstance(t, int) or t >= 2:
                    pe.wait_ge(xnT_ready, t - 1)
                    pe.wait_ge(er_out, t - 1)
                for k in range(K):
                    ins = turn(banks[u][:, k * P:(k + 1) * P], xn_t[0:P, u, k * 128:(k + 1) * 128], ident[0:P, 0:P])
                ins.then_inc(xn_turned, 1)

            def window(t, u):
                pe.wait_ge(xn_split, t + 1)
                hi, lo = xn_hi[:, u], xn_lo[:, u]
                for q in range(R // 2):
                    wait(pe, feat_out, R // 2 * t + q - 1)
                    for r in range(2):
                        for k in range(K):
                            ins = mm_parts(feat_ps[q % 2][0:P, r, :], hi[:, k, :], lo[:, k, :], w_hi[:, k, 2 * q + r, :],
                                           w_lo[:, k, 2 * q + r, :], k == 0, k == K - 1)
                    ins.then_inc(feat_done, 1)
                if isinstance(t, int) and t == 0:
                    pe.wait_ge(dst_folded, 1)
                for k in range(K):
                    ins = mm(banks[u][0:P, 256:256 + R * H], xnT_s[:, u, k, :], wer[:, k, :],
                             start=(k == 0), stop=(k == K - 1))
                ins.then_inc(er_done, 1)
                wait(pe, kv_normed, t)
                if isinstance(t, int) and t == 0:
                    pe.wait_ge(kv_split, 1)
                for i in range(2):
                    mm(banks[6][0:P, :], ones_r[:, 0:P], (bkv_hi, bkv_lo)[i][:, :], start=(i == 0), stop=False)
                for k in range(K):
                    ins = mm_parts(banks[6][0:P, :], hi[:, k, :], lo[:, k, :], wkv_hi[:, k, :], wkv_lo[:, k, :], False, k == K - 1)
                ins.then_inc(kv_done, 1)

            def sum_kv(t, u, first=False, last=False):
                if not first:
                    pe.wait_ge(kv_scaled, t + 1)
                for hb in range(K):
                    ins = mm(banks[7][:, hb * 128:(hb + 1) * 128], kv_s[0:P, u, hb * 128:(hb + 1) * 128],
                             kv_s[0:P, u, D + hb * 128:D + (hb + 1) * 128],
                             start=first and hb == 0, stop=last, skip_group_check=True)
                ins.then_inc(kv_summed, 1)

            def window_pair_pe(i, last=False):
                for u in range(2):
                    t = 2 * i + u
                    window(t, u)
                    sum_kv(t - 1, 1 - u, first=isinstance(t, int) and t == 0)
                    if not last:
                        turn_window(t + 2, u)

            pe.wait_ge(idents_ready, 1)
            turn_window(0, 0)
            turn_window(1, 1)
            pe.wait_ge(weights_ready, 1)
            for k in range(K):
                for hb in range(K):
                    ins = turn(banks[7][:, hb * D + k * 128:hb * D + (k + 1) * 128],
                               q_packed[:, k, hb * 128:(hb + 1) * 128], ident[:, :])
            ins.then_inc(wq_turned, 1)
            pe.wait_ge(wqT_ready, 1)
            pe.wait_ge(src_folded, 1)
            window_pair_pe(0)
            with pe.Fori(1, W // 2 - 1) as i:
                window_pair_pe(i)
            window_pair_pe(W // 2 - 1, last=True)
            sum_kv(W - 1, 1, last=True)

            pe.wait_ge(fold_ready, 1)
            pe.wait_ge(mixw_loaded, 16 * (2 + MH + K + FC))
            for hb in range(K):
                mm(banks[0][:, hb * D:(hb + 1) * D], kvd[:, hb, :], wqT[:, hb, :], start=(hb == 0), stop=True,
                   skip_group_check=True)
                ins = mm(banks[1][:, hb:hb + 1], kvd[:, hb, :], bq[:, hb:hb + 1], start=(hb == 0), stop=True,
                         skip_group_check=True)
            ins.then_inc(fold_mm, 1)
            pe.wait_ge(fold_ready, 3)
            for k in range(K):
                for hb in range(K):
                    mm(banks[2][:, k * D:(k + 1) * D], mixT[:, hb, k * 128:(k + 1) * 128], w1m[:, hb, :],
                       start=(k == 0 and hb == 0), stop=True, skip_group_check=True)
            for k in range(K):
                for hb in range(K):
                    ins = mm(banks[3][:, k:k + 1], w1m[:, hb, k * 128:(k + 1) * 128], cvec[:, hb:hb + 1],
                             start=(k == 0 and hb == 0), stop=True, skip_group_check=True)
            ins.then_inc(fold_mm, 1)
            pe.wait_ge(fold_ready, 4)
            pe.wait_ge(xnT_kept, W)

            def mix_block_h(b, u):
                if not isinstance(b, int) or b >= 2:
                    pe.wait_ge(mix_gelu, (b - 1) * K)
                for k in range(K):
                    for q in range(K):
                        ins = mm(banks[u * K + k][:, 0:BN], weff[:, q, k * 128:(k + 1) * 128],
                                 xnT[:, q, bass.ds(b * BN, BN)], start=(q == 0), stop=(q == K - 1))
                    ins.then_inc(mix_h, 1)

            def mix_block_out(b, u):
                pe.wait_ge(mix_gelu, (b + 1) * K)
                for i in range(BLK):
                    t = b * BLK + i
                    if not isinstance(b, int) or t >= 2:
                        pe.wait_ge(mix_added, t - 1)
                    for k in range(K):
                        ins = mm(banks[4 + (u * BLK + i) % 2][0:P, 0:D], hT_m[u][:, k, i * P:(i + 1) * P], w2m[:, k, :],
                                 start=(k == 0), stop=(k == K - 1))
                    ins.then_inc(mix_out, 1)

            def mix_pair(i, last=False):
                mix_block_h(2 * i + 1, 1)
                mix_block_out(2 * i, 0)
                if not last:
                    mix_block_h(2 * i + 2, 0)
                mix_block_out(2 * i + 1, 1)

            mix_block_h(0, 0)
            mix_pair(0)
            with pe.Fori(1, NB // 2 - 1) as i:
                mix_pair(i)
            mix_pair(NB // 2 - 1, last=True)

            pe.wait_ge(masks_ready, 1)
            pe.wait_ge(mix_added, W)
            pe.sem_inc(er_further, 1)
            pe.sem_inc(sum_further, 1)

            def sum_er(c, n, u, lo, up):
                v = u % 2
                wait(pe, carried, 2 * (c - 1))
                pe.wait_ge(pens_staged, c + 1)
                for q in range(2):
                    ins = turn(banks[2 + v][0:4, (2 + q) * P:(3 + q) * P], pens_now[0:P, u, q, :], ident[0:P, 0:P])
                ins.then_inc(pens_turned, 1)
                wait(pe, scores_done, c)
                pe.wait_ge(dhot_first, c + 1)
                pe.wait_ge(er_now_loaded[v], 16 * (n * (U // 2) + u // 2 + 1))
                for j in range(J):
                    for q in range(PIECES):
                        ins = mm(banks[0][0:P, j * R * H:(j + 1) * R * H], dhot[0][0:P, j * P:(j + 1) * P],
                                 er_now[0:P, v, q, :],
                                 start=(j == 0 and q == 0), stop=True, skip_group_check=True)
                ins.then_inc(er_first, 1)

                def er_of(w):
                    pe.wait_ge(dhot_further, w)
                    pe.wait_ge(er_far_loaded, 16 * w)
                    for j in range(J):
                        for q in range(PIECES):
                            ins = mm(banks[0][0:P, j * R * H:(j + 1) * R * H], dhot[1][0:P, j * P:(j + 1) * P],
                                     er_far[0:P, q, :],
                                     start=False, stop=True, skip_group_check=True)
                    ins.then_inc(er_further, 1)

                further(pe, lo, up, er_of)

            def turn_tails(c, n, u):
                v = u % 2
                pe.wait_ge(runs_ready, c + 1)
                pe.wait_ge(pens_copied, c + 1)
                turn(banks[2 + v][0:4, 0:P], runF[v][0:P, :, J - 1], ident[0:P, 0:P])
                turn(banks[2 + v][0:4, P:2 * P], runB[v][0:P, :, 0], ident[0:P, 0:P]).then_inc(tails_turned, 1)

            def turn_carry(c, n, u):
                v = u % 2
                pe.wait_ge(carried, 2 * (c + 1))
                wait(pe, diff_ready, c - 1)
                wait(pe, carry_ready, c - 1)
                settle(pe)
                turn(banks[4 + v][0:P, 0:H], gx[:, v, 0:P], ident[0:4, 0:4])
                turn(banks[4 + v][0:P, H:2 * H], hx[:, v, 1:P + 1], ident[0:4, 0:4]).then_inc(carry_back, 1)

            def spread_fac(c, u):
                pe.wait_ge(facdiag_ready, c + 1)
                pe.wait_ge(diff_ready, c + 1)
                mm(banks[4 + u % 2][:, 2 * H:3 * H], ones[0:4, :], facdiag[:, :], start=True, stop=True,
                   skip_group_check=True).then_inc(fac_spread, 1)

            def place_sums(c, u, lo, up):
                pe.wait_ge(ehot_first, c + 1)
                pe.wait_ge(scaled_vector, c + 1)
                pe.wait_ge(scaled_scalar, (J - JV) * H * (c + 1))
                wait(pe, kept_first, c - 1)
                for j in range(J):
                    mm(banks[6 + u % 2][0:P, 0:ROW], ehot[u % 2][0:P, j, :], slots[u][0:P, j, :], start=(j == 0), stop=True,
                       skip_group_check=True)
                pe.wait_ge(carry_ready, c + 1)
                wait(pe, kept_first, c)
                pe.wait_ge(kept_further, lo + 1)
                for h in range(H):
                    ins = mm(banks[6 + u % 2][0:1, h * HC:(h + 1) * HC], carry_sel[0:P, u % 2, h:h + 1],
                             summed[1 - u % 2][0:P, h * HC:(h + 1) * HC], start=False, stop=True, skip_group_check=True)
                ins.then_inc(sum_first, 1)

                def sum_of(w):
                    pe.wait_ge(ehot_further, w)
                    pe.wait_ge(kept_further, w)
                    for j in range(J):
                        ins = mm(banks[1][0:P, 0:ROW], ehot[2][0:P, j, :], slots[u][0:P, j, :],
                                 start=(j == 0), stop=(j == J - 1))
                    ins.then_inc(sum_further, 1)

                further(pe, lo, up, sum_of)

            def chunk_pe(c, n, u, win, load_next):
                turn_tails(c, n, u)
                if not isinstance(c, int) or c < NC - 1:
                    sum_er(c + 1, n + (u + 1) // U, (u + 1) % U, win[3], win[4])
                if not isinstance(c, int) or c >= 1:
                    spread_fac(c - 1, (u - 1) % U)
                turn_carry(c, n, u)
                load_next()
                if not isinstance(c, int) or c >= 1:
                    place_sums(c - 1, (u - 1) % U, win[1], win[2])

            first, second = (pe.value_load(hi[0:1, k:k + 1], min_val=0, max_val=W - 1) for k in range(2))
            sum_er(0, 0, 0, first, second)
            win = chunks(pe, chunk_pe, windows=True)
            spread_fac(NC - 1, (NC - 1) % U)
            place_sums(NC - 1, (NC - 1) % U, win[1], win[2])

            def turn_y(b, u):
                for i in range(BLK):
                    t = b * BLK + i
                    pe.wait_ge(y_ready, t + 1)
                    if not isinstance(b, int) or t >= 2:
                        pe.wait_ge(yT_ready, t - 1)
                    for k in range(K):
                        ins = turn(banks[6 + (u * BLK + i) % 2][:, k * P:(k + 1) * P], xn_t[0:P, i, k * 128:(k + 1) * 128],
                                   ident[0:P, 0:P])
                    ins.then_inc(y_turned, 1)

            def ffn_hidden(b, u):
                pe.wait_ge(xn_split, W + b + 1)
                if isinstance(b, int) and b == 0:
                    pe.wait_ge(ffnw_split, 1)
                for f in range(FC):
                    if not isinstance(b, int) or b * FC + f >= 4:
                        pe.wait_ge(ffn_gelu, b * FC + f - 3)
                    for k in range(K):
                        ins = mm_parts(banks[f % 4][:, 0:BNE], *(w[:, k, f * 128:(f + 1) * 128] for w in w1f_parts),
                                       y_hi[:, u, k, :], y_lo[:, u, k, :], k == 0, k == K - 1)
                    ins.then_inc(ffn_h, 1)

            def ffn_out(b, u):
                pe.wait_ge(hidden_split, b + 1)
                if isinstance(b, int) and b == 0:
                    pe.wait_ge(ffnw_split, 2)
                for i in range(BLK):
                    t = b * BLK + i
                    if not isinstance(b, int) or t >= 2:
                        pe.wait_ge(ffn_z_out, t - 1)
                    for f in range(FC):
                        ins = mm_parts(banks[4 + (u * BLK + i) % 2][0:P, 0:D], h_hi[u][:, f, i * P:(i + 1) * P],
                                       h_lo[:, u, f, i * P:(i + 1) * P], *(w[:, f, :] for w in w2f_parts), f == 0, f == FC - 1)
                    ins.then_inc(ffn_z, 1)

            def rank_ties():
                pe.wait_ge(tie_ready, 1)
                mm(banks[6][0:P, 0:W], upto[0:P, 0:P], tie[0:P, 0, :], start=True, stop=True, skip_group_check=True)
                mm(banks[6][0:P, W:2 * W], ones[0:P, 0:P], tie[0:P, 0, :], start=False, stop=True, skip_group_check=True)\
                    .then_inc(tie_ranked, 1)

            second_half(pe, turn_y, ffn_hidden, ffn_out, rank_ties)

        @block.vector
        def _(dve):
            v_ = nc.vector
            own = Steps(dve, vector_step, settle)

            own(v_.memset(headmask[:, :], 0.0))
            for q in range(128 // MD):
                ins = v_.memset(headmask[q * MD:(q + 1) * MD, q * MD:(q + 1) * MD], 1.0 / N)
            own(ins)

            stat_own = Steps(dve, stat_step, settle)
            inv_own = Steps(dve, inv_step, settle)

            def row_stats(k, t, n):
                stat_own.at(3 * k)
                for u in range(n):
                    ins = v_.bn_stats(stats[0:P, u, :], x_sb[0:P, bass.ds(t + u, 1), :].rearrange("p w d -> p (w d)"))
                stat_own(ins)
                for u in range(n):
                    ins = v_.bn_aggr(mv2[0:P, u, :], stats[0:P, u, :])
                stat_own(ins)
                stat_own(v_.tensor_copy(mv[0:P, bass.ds(t, n), :], mv2[0:P, 0:n, :]))
                dve.sem_inc(var_ready, 1)

            def invert_std(k, t, n):
                dve.wait_ge(std_ready, k + 1)
                inv_own.at(k)
                inv_own(v_.reciprocal(rstd[0:P, bass.ds(t, n)], rstd[0:P, bass.ds(t, n)]))

            def normalise(t, u):
                if not isinstance(t, int) or t >= 2:
                    dve.wait_ge(xn_turned, t - 1)
                    dve.wait_ge(xn_added, t - 1)
                v_.tensor_scalar(xn_t[0:P, u, :], x_sb[0:P, bass.ds(t, 1), :].rearrange("p w d -> p (w d)"),
                                 mv[0:P, bass.ds(t, 1), 0:1].rearrange("p w o -> p (w o)"), rstd[0:P, bass.ds(t, 1)],
                                 ALU.subtract, ALU.mult).then_inc(xn_ready, 1)

            dve.wait_ge(x_loaded[0], 32)
            row_stats(0, 0, AHEAD)
            invert_std(0, 0, AHEAD)
            for u in range(2):
                normalise(u, u)

            split_own = Steps(dve, split_step, settle)

            def split_window(t, u):
                dve.wait_ge(xnT_ready, t + 1)
                split_own.at(K + t)
                split_own(v_.tensor_copy(xn_hi[:, u], xnT_s[:, u]))
                v_.tensor_tensor(xn_lo[:, u], xnT_s[:, u], xn_hi[:, u].bitcast(F32), ALU.subtract).then_inc(xn_split, 1)

            def fold_src(k):
                dve.wait_ge(conv_loaded[k], 16)
                dve.wait_ge(attn_loaded[0], 16)
                cols = waug[:, k, :, :].rearrange("p r (h c) -> p (r h) c", c=HC)
                own(v_.tensor_tensor(src_prod, cols[:, :, 0:HD], attn_b[0], ALU.mult))
                own(v_.tensor_reduce(cols[:, :, HD], src_prod, AX.X, ALU.add))
                dve.sem_inc(src_fold, 1)

            def split_weights(k):
                dve.wait_ge(dst_products, k + 1)
                dve.wait_ge(w_hi_ready, k + 1)
                split_own(v_.tensor_tensor(w_lo[:, k], waug[:, k], w_hi[:, k].bitcast(F32), ALU.subtract))

            def fold_dst():
                dve.wait_ge(dst_products, K)
                for k in range(K):
                    ins = v_.tensor_reduce(wer[:, k, :], dst_prod[k], AX.X, ALU.add)
                ins.then_inc(dst_folded, 1)

            fold_src(0)

            dve.wait_ge(qkv_loaded, 32)
            heads = wqkv.rearrange("p k (h s d) -> p k h s d", s=3, d=MD)
            for k in range(K):
                ins = v_.tensor_reduce(var16[:, k, :].rearrange("p (h s) -> p h s", s=2), heads[:, k, :, 1:3, :], AX.X, ALU.add)
            own(ins)
            for k in range(K):
                for i in range(2):
                    ins = v_.scalar_tensor_tensor(
                        wkv[:, k, i * D:(i + 1) * D].rearrange("p (h d) -> p h d", d=MD),
                        var16[:, k, :].rearrange("p (h s) -> p h s", s=2)[:, :, i].unsqueeze(2).to_broadcast([128, MH, MD]),
                        -1.0 / MD, heads[:, k, :, 1 + i, :], ALU.mult, ALU.add)
            own(ins)
            bheads = brow.rearrange("p (h s d) -> p h s d", s=3, d=MD)
            own(v_.tensor_reduce(var16[0:1, 0, :].rearrange("p (h s) -> p h s", s=2), bheads[:, :, 1:3, :], AX.X, ALU.add))
            for i in range(2):
                ins = v_.scalar_tensor_tensor(
                    bkv[:, i * D:(i + 1) * D].rearrange("p (h d) -> p h d", d=MD),
                    var16[0:1, 0, :].rearrange("p (h s) -> p h s", s=2)[:, :, i].unsqueeze(2).to_broadcast([1, MH, MD]),
                    -1.0 / MD, bheads[:, :, 1 + i, :], ALU.mult, ALU.add)
            own(ins)

            dve.sem_inc(kv_centred, 1)
            split_weights(0)
            fold_src(1)
            split_weights(1)
            dve.sem_inc(src_folded, 1)
            for u in range(2):
                split_window(u, u)
            dve.wait_ge(kv_hi_ready, 1)
            v_.tensor_tensor(wkv_lo[:, :, :], wkv, wkv_hi[:, :, :].bitcast(F32), ALU.subtract)
            v_.tensor_tensor(bkv_lo[:, :], bkv[:, :], bkv_hi[:, :].bitcast(F32), ALU.subtract)
            dve.wait_ge(idents_ready, 1)
            v_.tensor_copy(ones_r[:, :], ones[0:1, :]).then_inc(kv_split, 1)
            v_.memset(summed[0][0:P], 0.0)
            v_.memset(summed[1][0:P], 0.0).then_inc(zeros_ready, 1)

            er_own = Steps(dve, er_step, settle)

            def window_pair_dve(i, last=False, stats=True):
                for u in range(2):
                    t = 2 * i + u
                    if u == 0 and not (isinstance(i, int) and i == 0):
                        split_window(t + 1, 1)
                    if u == 1 and not last:
                        split_window(t + 1, 0)
                    if isinstance(t, int) and t == 0:
                        fold_dst()
                    if u == 0 and not last and not (isinstance(i, int) and i == 0):
                        invert_std(i, 2 * i + 2, 2)
                    if not last:
                        normalise(t + 2, u)
                    if stats and u == 0:
                        row_stats(i + 1, 2 * i + AHEAD, 2)
                    dve.wait_ge(er_done, t + 1)
                    v_.tensor_copy(er_row[0:P, 0, :], banks[u][0:P, 256:256 + R * H]).then_inc(er_out, 1)
                    dve.wait_ge(er_out, t + 1)
                    wait(dve, er_written[u], 16 * i)
                    er_own.at(4 * t)
                    for q in range(PIECES - 1):
                        er_own(v_.tensor_copy(er_out_row[0:P, u, q, :], er_row[0:P, q, :]))
                        er_own(v_.tensor_tensor(er_row[0:P, q + 1, :], er_row[0:P, q, :], er_out_row[0:P, u, q, :], ALU.subtract))
                    v_.tensor_copy(er_out_row[0:P, u, PIECES - 1, :], er_row[0:P, PIECES - 1, :]).then_inc(er_split, 1)
                    dve.wait_ge(sq_ready, t + 1)
                    v_.tensor_reduce(var16[0:P, 0, :], sq[0:P].rearrange("p (q d) -> p q d", d=MD), AX.X, ALU.add)\
                      .then_inc(kvar_ready, 1)
                    dve.wait_ge(kstd_ready, t + 1)
                    v_.reciprocal(var16[0:P, 1, :], var16[0:P, 1, :]).then_inc(krstd_ready, 1)
                    dve.wait_ge(krstd_ready, t + 1)
                    wait(dve, kv_summed, t)
                    v_.tensor_tensor(kv_s[0:P, u, :].rearrange("p (q d) -> p q d", d=MD),
                                     banks[6][0:P, :].rearrange("p (q d) -> p q d", d=MD),
                                     var16[0:P, 1, :].unsqueeze(2).to_broadcast([P, 2 * MH, MD]), ALU.mult)\
                      .then_inc(kv_normed, 1)

            def count_places():
                step = Steps(dve, sort_step, settle)
                step(v_.scalar_tensor_tensor(key[0:P], dst10[0:P, :, 1:J + 1], float(1 << 6), iota[0:P, 0:NC].unsqueeze(2)
                                             .to_broadcast([P, NC, J]), ALU.mult, ALU.add))
                dve.sem_inc(keys_ready, 1)
                dve.sem_inc(key_row_used, 1)
                step(v_.memset(rank[0:P], 1.0))
                dve.wait_ge(places_ready, 1)
                whole, tied = 3 * J // 2, 5 * J
                with dve.Fori(0, NC) as piece:
                    dve.wait_ge(key_row_loaded, 16 * (piece + 1))
                    settle(dve)
                    before = 2 + piece * (NC * whole + tied)

                    def count(c, j0, n, flags):
                        step(v_.tensor_reduce(fewer[0:P, 0:n], flags, AX.X, ALU.add))
                        at = rank[0:P, bass.ds(c, 1), j0:j0 + n].rearrange("p c j -> p (c j)")
                        step(v_.tensor_tensor(at, at, fewer[0:P, 0:n], ALU.add))

                    def against(flags, row, column, n, op):
                        step(v_.tensor_tensor(flags, row[0:P].unsqueeze(1).to_broadcast([P, n, CH]),
                                              column.unsqueeze(2).to_broadcast([P, n, CH]), op))

                    with dve.Fori(0, NC) as c:
                        step.at(before + c * whole)
                        for j0 in range(0, J, 2):
                            against(less[0:P], key_row, key[0:P, bass.ds(c, 1), j0:j0 + 2].rearrange("p c j -> p (c j)"), 2, ALU.is_lt)
                            count(c, j0, 2, less[0:P])
                    step.at(before + NC * whole)
                    for j in range(J):
                        same_key, earlier = less[0:P, 0:1], less[0:P, 1:2]
                        against(same_key, key_row, key[0:P, bass.ds(piece, 1), j:j + 1].rearrange("p c j -> p (c j)"), 1, ALU.is_equal)
                        against(earlier, place_row, place_col[0:P, j:j + 1], 1, ALU.is_lt)
                        step(v_.tensor_tensor(same_key, same_key, earlier, ALU.mult))
                        count(piece, j, 1, same_key)
                    dve.sem_inc(key_row_used, 1)
                step.at(2 + NC * (NC * whole + tied))

                def stage_edges(c):
                    for q, of in enumerate((rank, dst10[:, :, 1:J + 1], src_t, typ_t)):
                        ins = v_.tensor_copy(edge_now[0:P, q, :], of[0:P, bass.ds(c, 1), :].rearrange("p c j -> p (c j)"))
                    ins.then_inc(edge_staged, 1)

                stage_edges(0)
                with dve.Fori(1, NC) as c:
                    dve.wait_ge(edge_scattered, 16 * 3 * J * c)
                    settle(dve)
                    stage_edges(c)
                dve.wait_ge(edges_loaded, 128)

            def sort_edges():
                dve.wait_ge(edges_loaded, 64)
                own(v_.tensor_tensor(descent[0:P], dst10[0:P, :, 0:J], dst10[0:P, :, 1:J + 1], ALU.is_gt))
                v_.tensor_reduce(descents[0:P, :], descent[0:P], AX.XY, ALU.max).then_inc(descents_ready, 1)
                v_.memset(penF[0:P, :, :, 0], NEG)
                v_.memset(penB[0:P, :, :, 0], NEG)
                dve.wait_ge(descents_loaded, 16)
                own(v_.tensor_reduce(unsorted_f[:, :], descents_row[:, :], AX.X, ALU.max))
                v_.tensor_copy(unsorted[:, :], unsorted_f[:, :]).then_inc(unsorted_ready, 1)
                dve.wait_ge(unsorted_ready, 1)
                settle(dve)
                with dve.If(dve.value_load(unsorted[0:1, 0:1], min_val=0, max_val=1) > 0):
                    count_places()
                v_.scalar_tensor_tensor(row_idx[0:P], src_t[0:P], float(R), typ_t[0:P], ALU.mult, ALU.add).then_inc(idx_ready, 1)
                own(v_.tensor_copy(dstf[0:P], dst10[0:P]))
                v_.tensor_copy(first_node[:, :], ends[0:1, 0:NC])
                own(v_.tensor_copy(endsf[0:P], ends[0:P]))

            def prepare_edges():
                own(v_.tensor_tensor(pen[0:P], dstf[0:P, :, 1:J + 2], dstf[0:P, :, 0:J + 1], ALU.is_equal))
                own(v_.tensor_scalar(pen[0:P], pen[0:P], -1.0, -NEG, ALU.add, ALU.mult))
                v_.tensor_copy(penF[0:P, :, :, 1:J], pen[0:P, :, 1:J].unsqueeze(2).to_broadcast([P, NC, H, J - 1]))
                for j in range(1, J):
                    v_.tensor_copy(penB[0:P, :, :, j], pen[0:P, :, J - j].unsqueeze(2).to_broadcast([P, NC, H]))
                v_.tensor_copy(penA[0:P, :, 0], pen[0:P, :, 0])
                own(v_.tensor_copy(penZ[0:P, :, J - 1], pen[0:P, :, J]))
                for j in range(1, J):
                    v_.tensor_tensor(penA[0:P, :, j], penA[0:P, :, j - 1], pen[0:P, :, j], ALU.min)
                    own(v_.tensor_tensor(penZ[0:P, :, J - 1 - j], penZ[0:P, :, J - j], pen[0:P, :, J - j], ALU.min))
                v_.tensor_copy(pen0[0:P], penA[0:P, :, J - 1].unsqueeze(2).to_broadcast([P, NC, H]))
                own(v_.tensor_copy(pen1[0:P], penZ[0:P, :, 0].unsqueeze(2).to_broadcast([P, NC, H])))
                first, last = endsf[0:P, 0:NC], endsf[0:P, NC:2 * NC]
                own(v_.tensor_tensor(spread[0:P], last, first, ALU.subtract))
                own(v_.tensor_tensor(hi_cmp[0:P], spread[0:P].unsqueeze(2).to_broadcast([P, NC, W]),
                                     wbase[0:P, :].unsqueeze(1).to_broadcast([P, NC, W]), ALU.is_ge))
                own(v_.tensor_reduce(lastrow[0:P, 1:], hi_cmp[0:P], AX.X, ALU.add))
                own(v_.tensor_scalar(lastrow[0:P, 1:], lastrow[0:P, 1:], -1.0, None, ALU.add))
                v_.memset(hi_f[0:P, 0:1], 0.0)
                own(v_.tensor_tensor_scan(hi_f[0:P, 1:NC + 1], ones[0:P, 0:NC], lastrow[0:P, 1:], 0.0, ALU.mult, ALU.add))
                v_.tensor_copy(hi_f[0:P, NC + 1:], hi_f[0:P, NC:NC + 1].to_broadcast([P, 3]))
                own(v_.scalar_tensor_tensor(lastrow[0:P, 1:], lastrow[0:P, 1:], -float(P), spread[0:P], ALU.mult, ALU.add))
                v_.memset(same[0:P, 0:1], 0.0)
                v_.memset(lastrow[0:P, 0:1], -1.0)
                own(v_.tensor_tensor(same[0:P, 1:NC], endsf[0:P, 1:NC], endsf[0:P, NC:2 * NC - 1], ALU.is_equal))
                own(v_.scalar_tensor_tensor(rowhot[0:P, :], lastrow[0:P, 0:NC], pcolf[0:P, :], same[0:P, 0:NC],
                                            ALU.is_equal, ALU.mult))
                v_.tensor_scalar(node[0:P, :], first, pcolf[0:P, :], None, ALU.add)
                v_.tensor_tensor(dloc[0:P], dstf[0:P, :, 1:J + 1], first.unsqueeze(2).to_broadcast([P, NC, J]), ALU.subtract)
                own(v_.tensor_copy(hi[:, :], hi_f[0:1, :]))
                dve.sem_inc(masks_ready, 1)

            dve.wait_ge(x_loaded[1], 32)
            window_pair_dve(0)
            sort_edges()
            prepare_edges()
            dve.wait_ge(x_loaded[2], 32)
            with dve.Fori(1, W // 2 - 2) as i:
                window_pair_dve(i)
            window_pair_dve(W // 2 - 2, stats=False)
            window_pair_dve(W // 2 - 1, last=True, stats=False)

            own(v_.tensor_tensor(rel_hot[0:P].rearrange("p c j r -> p (c j) r"),
                                 typ_t[0:P].rearrange("p c j -> p (c j)").unsqueeze(2).to_broadcast([P, NC * J, R]),
                                 iota[0:P, 0:R].unsqueeze(1).to_broadcast([P, NC * J, R]), ALU.is_equal))

            dve.wait_ge(kv_summed, W + 1)
            v_.tensor_tensor(kvd, banks[7][:, 0:D].rearrange("p (k n) -> p k n", k=K),
                             headmask[:, :].unsqueeze(1).to_broadcast([128, K, 128]), ALU.mult).then_inc(fold_ready, 1)
            dve.wait_ge(fold_mm, 1)
            own(v_.tensor_copy(mixT, banks[0].rearrange("p (k n) -> p k n", k=K)))
            v_.tensor_copy(cvec, banks[1][:, 0:K]).then_inc(fold_ready, 1)
            for hb in range(K):
                diag = mixT[:, hb, hb * 128:(hb + 1) * 128]
                ins = v_.tensor_tensor(diag, diag, ident[:, :], ALU.add)
            ins.then_inc(fold_ready, 1)
            dve.wait_ge(fold_mm, 2)
            v_.tensor_copy(weff, banks[2].rearrange("p (k n) -> p k n", k=K))
            v_.tensor_tensor(beff[:, :], banks[3][:, 0:K], b1m[:, :], ALU.add).then_inc(fold_ready, 1)

            def mix_add(b, u):
                for i in range(BLK):
                    t = b * BLK + i
                    dve.wait_ge(mix_out, t + 1)
                    rows = x_sb[0:P, bass.ds(t, 1), :].rearrange("p w d -> p (w d)")
                    v_.tensor_tensor(rows, rows, banks[4 + (u * BLK + i) % 2][0:P, 0:D], ALU.add).then_inc(mix_added, 1)

            dve.wait_ge(xn_added, W)
            with dve.Fori(0, NB // 2) as i:
                for u in range(2):
                    mix_add(2 * i + u, u)

            spread_own = Steps(dve, spread_step)
            spare_dve = dve.alloc_register("spare_dve")

            def spread_dst(c, n, u, lo, up):
                edges = dst_row[u % 2][0:P].rearrange("n (p j) -> n j p", j=J)
                dve.wait_ge(dst_row_loaded[u % 2], 16 * (n * (U // 2) + u // 2 + 1))
                v_.tensor_scalar(dhot[0][0:P].rearrange("n (j p) -> n j p", j=J), edges, node[0:P, bass.ds(c, 1)], None,
                                 ALU.is_equal).then_inc(dhot_first, 1)

                def spread_window(w):
                    dve.wait_ge(er_further, w)
                    spread_own.at(w - 1)
                    spread_own(v_.tensor_tensor(node_further[0:P, 0, :], node[0:P, bass.ds(c, 1)],
                                                wbase[0:P, bass.ds(within(dve, spare_dve, w - lo, W - 1), 1)], ALU.add))
                    v_.tensor_scalar(dhot[1][0:P].rearrange("n (j p) -> n j p", j=J), edges, node_further[0:P, 0, :],
                                     None, ALU.is_equal).then_inc(dhot_further, 1)

                further(dve, lo, up, spread_window)

            score_own = Steps(dve, score_step)
            carry_own = Steps(dve, carry_step)
            weight_own = Steps(dve, weight_step)
            place_further_own = Steps(dve, place_further_step)

            def now(of, c):
                part = of[0:P, bass.ds(c, 1)]
                return part.rearrange("p c h j -> p (c h) j") if len(part.shape) == 4 else part.rearrange("p c j -> p (c j)")

            def scores(c, n, u, up):
                v = u % 2
                score_own.at(3 * c)
                dve.wait_ge(er_first, c + 1)
                dve.wait_ge(er_further, up + 1)
                v_.tensor_tensor(ersel[0:P], banks[0][0:P, 0:J * R * H].rearrange("p (j r h) -> p j h r", j=J, r=R),
                                 now(rel_hot, c).unsqueeze(2).to_broadcast([P, J, H, R]), ALU.mult).then_inc(scores_done, 1)
                dve.wait_ge(scores_done, c + 1)
                score_own(v_.tensor_reduce(er_e[0:P], ersel[0:P], AX.X, ALU.add))
                dve.wait_ge(gathered[u], 16 * J * (n + 1))
                el = slots[u][0:P].rearrange("p j (h c) -> p h j c", c=HC)[:, :, :, HD]
                score_own(v_.tensor_tensor(score[0:P], er_e[0:P].rearrange("p j h -> p h j"), el, ALU.add))
                v_.memset(slots[u][0:P].rearrange("p j (h c) -> p (j h) c", c=HC)[:, :, HD:HC], 1.0)
                score_own(v_.scalar_tensor_tensor(e_cur[0:P, v], score[0:P], 0.2, score[0:P], ALU.mult, ALU.max))
                e = e_cur[0:P, v].rearrange("p h j -> p (h j)")
                v_.tensor_tensor_scan(runF[v][0:P].rearrange("p h j -> p (h j)"), now(penF, c).rearrange("p h j -> p (h j)"),
                                      e, NEG, ALU.add, ALU.max)
                ins = v_.tensor_tensor_scan(reverse(runB[v][0:P].rearrange("p h j -> p (h j)")),
                                            now(penB, c).rearrange("p h j -> p (h j)"), reverse(e),
                                            NEG, ALU.add, ALU.max)
                ins.then_inc(runs_ready, 1)

            def carry(c, n, u):
                v = u % 2
                carry_own.at(c)
                dve.wait_ge(tails_turned, c + 1)
                tails = banks[2 + v][0:4]
                v_.tensor_copy(gx[:, v, 0:1], gx[:, 1 - v, P:P + 1])
                v_.tensor_tensor_scan(gx[:, v, 1:P + 1], penT[:, v, 0:P], tails[:, 0:P], gx[:, 1 - v, P:P + 1],
                                      ALU.add, ALU.max).then_inc(carried, 1)
                v_.tensor_tensor_scan(reverse(hx[:, v, 0:P]), reverse(penT[:, v, P:2 * P]), reverse(tails[:, P:2 * P]), NEG,
                                      ALU.add, ALU.max).then_inc(carried, 1)
                dve.wait_ge(carried, 2 * (c + 1))
                carry_own(v_.tensor_tensor(fac[:, 0:1], gx[:, v, 0:1], hx[:, v, 0:1], ALU.max))
                v_.tensor_tensor(fac[:, 1:2], gx[:, v, 0:1], fac[:, 0:1], ALU.subtract).then_inc(fac_diff, 1)

            def spread_factors(c):
                dve.wait_ge(fac_exp, c + 1)
                v_.tensor_scalar(facdiag[:, :], ident[0:4, 0:4], fac[:, 2:3], None, ALU.mult)\
                  .then_inc(facdiag_ready, 1)

            def weights(c, u):
                v = u % 2
                weight_own.at(2 * c)
                dve.wait_ge(carry_back, c + 1)
                weight_own(v_.tensor_tensor(
                    cmx[v][0:P, 0:2], banks[4 + v][0:P, 0:2 * H].rearrange("p (q h) -> p q h", q=2).unsqueeze(3)
                    .to_broadcast([P, 2, H, J]), penAZ[0:P, bass.ds(c, 1)].rearrange("p c q j -> p (c q) j").unsqueeze(2)
                    .to_broadcast([P, 2, H, J]), ALU.add))
                weight_own(v_.tensor_reduce(peak[0:P], cmx[v][0:P].rearrange("p q h j -> p h j q"), AX.X, ALU.max))
                v_.tensor_tensor(diff[0:P, v], e_cur[0:P, v], peak[0:P], ALU.subtract).then_inc(diff_ready, 1)

            def scale(c, u):
                dve.wait_ge(ex_ready, c + 1)
                part = slots[u][0:P, 0:JV].rearrange("p j (h c) -> p j h c", c=HC)
                v_.tensor_tensor(part, part, ex[0:P, u, :, 0:JV].rearrange("p h j -> p j h").unsqueeze(3)
                                 .to_broadcast([P, JV, H, HC]), ALU.mult).then_inc(scaled_vector, 1)

            def place(c, u):
                wait(dve, sum_first, c - 1)
                v_.tensor_tensor(ehot[u % 2][0:P], iota[0:P, :].unsqueeze(1).to_broadcast([P, J, P]),
                                 now(dloc, c).unsqueeze(2).to_broadcast([P, J, P]), ALU.is_equal).then_inc(ehot_first, 1)

            def hand_on(c, u, lo, up):
                dve.wait_ge(fac_spread, c + 1)
                v_.tensor_scalar(carry_sel[0:P, u % 2, :], banks[4 + u % 2][0:P, 2 * H:3 * H], rowhot[0:P, bass.ds(c, 1)],
                                 None, ALU.mult).then_inc(carry_ready, 1)

                def place_span(w):
                    dve.wait_ge(sum_further, w)
                    place_further_own.at(w - 1)
                    place_further_own(v_.tensor_scalar(dloc_further[0:P, 0, :], now(dloc, c), wbase[0:P, bass.ds(within(dve, spare_dve, w - lo, W - 1), 1)],
                                                       None, ALU.subtract))
                    v_.tensor_tensor(ehot[2][0:P], iota[0:P, :].unsqueeze(1).to_broadcast([P, J, P]),
                                     dloc_further[0:P, 0, :].unsqueeze(2).to_broadcast([P, J, P]), ALU.is_equal)\
                      .then_inc(ehot_further, 1)

                further(dve, lo, up, place_span)

            def chunk_dve(c, n, u, win, load_next):
                before = (u - 1) % U
                scores(c, n, u, win[3])
                if not isinstance(c, int) or c >= 2:
                    hand_on(c - 2, (u - 2) % U, win[0], win[1])
                if not isinstance(c, int) or c >= 1:
                    spread_factors(c - 1)
                    weights(c - 1, before)
                if not isinstance(c, int) or c < NC - 1:
                    spread_dst(c + 1, n + (u + 1) // U, (u + 1) % U, win[3], win[4])
                if not isinstance(c, int) or c >= 1:
                    place(c - 1, before)
                    scale(c - 1, before)
                load_next()
                carry(c, n, u)

            v_.memset(gx[:, 1, P:P + 1], NEG)
            own(v_.memset(hx[:, :, P:P + 1], NEG))
            first, second = (dve.value_load(hi[0:1, k:k + 1], min_val=0, max_val=W - 1) for k in range(2))
            spread_dst(0, 0, 0, first, second)
            win = chunks(dve, chunk_dve, windows=True)
            last = (NC - 1) % U
            hand_on(NC - 2, last - 1, win[0], win[1])
            spread_factors(NC - 1)
            weights(NC - 1, last)
            place(NC - 1, last)
            scale(NC - 1, last)
            hand_on(NC - 1, last, win[1], win[2])

            x2_own = Steps(dve, x2_step, settle)
            norm_own = Steps(dve, norm_step, settle)
            dve.wait_ge(wr_loaded, 32)

            def join(b, u):
                x2_own.at(6 * b)
                block = acc[0:P, bass.ds(b * BLK, BLK), :].rearrange("p w (h c) -> p (w h) c", c=HC)
                rden = rdens[0:P, u * BLK * H:(u + 1) * BLK * H]
                x2_own(v_.tensor_scalar(rden, block[:, :, HD], 1e-30, None, ALU.max))
                x2_own(v_.reciprocal(rden, rden))
                sums = block[:, :, 0:HD]
                x2_own(v_.tensor_tensor(sums, sums, rden.unsqueeze(2).to_broadcast([P, BLK * H, HD]), ALU.mult))
                rows = x_sb[0:P, bass.ds(b * BLK, BLK), :].rearrange("p w (h d) -> p (w h) d", d=HD)
                x2_own(v_.tensor_tensor(rows, rows, sums, ALU.add))
                for i in range(BLK):
                    ins = v_.bn_stats(stats[0:P, i, :], x_sb[0:P, bass.ds(b * BLK + i, 1), :].rearrange("p w d -> p (w d)"))
                x2_own(ins)
                for i in range(BLK):
                    ins = v_.bn_aggr(mv[0:P, u * BLK + i, :], stats[0:P, i, :])
                x2_own(ins)
                dve.sem_inc(x2_var, 1)

            def norm_y(b, u):
                dve.wait_ge(x2_std, b + 1)
                norm_own.at(2 * b)
                norm_own(v_.reciprocal(rstd[0:P, u * BLK:(u + 1) * BLK], rstd[0:P, u * BLK:(u + 1) * BLK]))
                for i in range(BLK):
                    t = b * BLK + i
                    if not isinstance(b, int) or b >= 1:
                        dve.wait_ge(y_turned, t - BLK + 1)
                        dve.wait_ge(y_added, t - BLK + 1)
                    v_.tensor_scalar(xn_t[0:P, i, :], x_sb[0:P, bass.ds(t, 1), :].rearrange("p w d -> p (w d)"),
                                     mv[0:P, u * BLK + i, 0:1], rstd[0:P, u * BLK + i:u * BLK + i + 1],
                                     ALU.subtract, ALU.mult).then_inc(y_ready, 1)
                dve.wait_ge(y_ready, (b + 1) * BLK)
                norm_own(v_.tensor_tensor(products[0:P], xn_t[0:P, :, :],
                                          bias_rows[0:P, 1, :].unsqueeze(1).to_broadcast([P, BLK, D]), ALU.mult))
                v_.tensor_reduce(wcol[0:P, bass.ds(b * BLK, BLK)], products[0:P], AX.X, ALU.add).then_inc(gated, 1)

            def split_y(b, u):
                dve.wait_ge(yT_ready, (b + 1) * BLK)
                split_own.at(K + W + b)
                split_own(v_.tensor_copy(y_hi[:, u], y_f[:, u]))
                v_.tensor_tensor(y_lo[:, u], y_f[:, u], y_hi[:, u].bitcast(F32), ALU.subtract).then_inc(xn_split, 1)

            def split_hidden(b, u):
                for f in range(0, FC, 2):
                    dve.wait_ge(ffn_gelu, b * FC + f + 2)
                    ins = v_.tensor_tensor(h_lo[:, u, f:f + 2, :], hT_f[u][:, f:f + 2, :], h_hi[u][:, f:f + 2, :].bitcast(F32),
                                           ALU.subtract)
                ins.then_inc(hidden_split, 1)

            def split_ffnw(i):
                dve.wait_ge(ffnw_hi_ready, i + 1)
                part = slice(i * K * F, (i + 1) * K * F)
                v_.tensor_tensor(ffnw_lo[:, part], ffnw[:, part], ffnw_hi[:, part].bitcast(F32), ALU.subtract).then_inc(ffnw_split, 1)

            dve.wait_ge(sums_loaded[0], 32)
            own(v_.memset(y_f[:, :, :, BN:], 0.0))
            join(0, 0)
            join(1, 1)
            split_ffnw(0)
            norm_y(0, 0)
            split_y(0, 0)
            split_ffnw(1)
            dve.wait_ge(sums_loaded[1], 32)
            join(2, 0)
            norm_y(1, 1)
            split_y(1, 1)

            def ffn_pair(i, last=False):
                split_hidden(2 * i, 0)
                join(2 * i + 3, 1)
                norm_y(2 * i + 2, 0)
                split_y(2 * i + 2, 0)
                if not last:
                    join(2 * i + 4, 0)
                norm_y(2 * i + 3, 1)
                split_y(2 * i + 3, 1)
                split_hidden(2 * i + 1, 1)

            ffn_pair(0)
            with dve.Fori(1, NB // 2 - 2) as i:
                ffn_pair(i)
            ffn_pair(NB // 2 - 2, last=True)
            split_hidden(NB - 2, 0)

            top = Steps(dve, topk_step, settle)
            dve.wait_ge(gated, NB)
            top(v_.tensor_scalar(wcol[0:P, :], wcol[0:P, :], br[0:P, :], None, ALU.add))
            top(v_.memset(prefix[:, :], 0))

            def as_float(key, bits, mask):
                top(v_.tensor_scalar(mask, key, 31, -1, ALU.arith_shift_right, ALU.bitwise_xor))
                top(v_.tensor_scalar(mask, mask, -2 ** 31, None, ALU.bitwise_or))
                top(v_.tensor_tensor(bits, key, mask, ALU.bitwise_xor))

            for r in range(ROUNDS):
                if r == ROUNDS // 2:
                    split_hidden(NB - 1, 1)
                shift = 32 - DIGIT * (r + 1)
                top(v_.tensor_scalar(cand[:, 0, :], digit[:, :], shift, None, ALU.logical_shift_left))
                top(v_.tensor_tensor(cand[:, 0, :], cand[:, 0, :], prefix[:, :].to_broadcast([128, CANDS - 1]), ALU.bitwise_or))
                as_float(cand[:, 0, :], cand[:, 1, :], cand[:, 2, :])
                top(v_.tensor_tensor(compared[0:P], wcol[0:P, :].unsqueeze(1).to_broadcast([P, CANDS - 1, W]),
                                     cand[0:P, 1, :].bitcast(F32).unsqueeze(2).to_broadcast([P, CANDS - 1, W]), ALU.is_ge))
                v_.tensor_reduce(count[0:P, :], compared[0:P], AX.X, ALU.add).then_inc(counted, 1)
                dve.wait_ge(totalled, r + 1)
                top(v_.tensor_scalar(reached[:, :], total[:, :], float(TOPK), 0.0, ALU.is_ge, ALU.add, accum_out=found[:, :]))
                top(v_.tensor_copy(foundi[:, :], found[:, :]))
                top(v_.tensor_scalar(foundi[:, :], foundi[:, :], shift, None, ALU.logical_shift_left))
                top(v_.tensor_tensor(prefix[:, :], prefix[:, :], foundi[:, :], ALU.bitwise_or))
            as_float(prefix[:, :], cand[:, 1, 0:1], cand[:, 2, 0:1])
            limit = cand[0:P, 1, 0:1].bitcast(F32)

            v_.tensor_scalar(tie[0:P, 0, :], wcol[0:P, :], limit, None, ALU.is_equal).then_inc(tie_ready, 1)
            top(v_.tensor_scalar(wsel[0:P, :], wcol[0:P, :], limit, None, ALU.is_gt))
            v_.tensor_reduce(count[0:P, 0:1], wsel[0:P, :], AX.X, ALU.add).then_inc(counted, 1)
            dve.wait_ge(totalled, ROUNDS + 1)
            top(v_.tensor_scalar(left[:, 0:1], total[:, 0:1], -1.0, float(TOPK), ALU.mult, ALU.add))
            dve.wait_ge(tie_ranked, 1)
            top(v_.tensor_copy(tie[0:P, 3, :], banks[6][0:P, W:2 * W]))
            top(v_.tensor_tensor_scan(tie[0:P, 1, :], ones[0:P, 0:W], tie[0:P, 3, :], 0.0, ALU.mult, ALU.add))
            top(v_.tensor_tensor(tie[0:P, 1, :], tie[0:P, 1, :], tie[0:P, 3, :], ALU.subtract))
            top(v_.tensor_tensor(tie[0:P, 1, :], tie[0:P, 1, :], banks[6][0:P, 0:W], ALU.add))
            top(v_.scalar_tensor_tensor(tie[0:P, 2, :], tie[0:P, 1, :], left[0:P, 0:1], tie[0:P, 0, :], ALU.is_le, ALU.mult))
            top(v_.tensor_tensor(wsel[0:P, :], wsel[0:P, :], tie[0:P, 2, :], ALU.add))
            top(v_.tensor_tensor(wsel[0:P, :], wsel[0:P, :], wcol[0:P, :], ALU.mult))

            dve.wait_ge(y_added, W)
            with dve.Fori(0, W) as t:
                dve.wait_ge(ffn_z_bias, t + 1)
                rows = acc[0:P, bass.ds(t, 1), 0:D].rearrange("p w d -> p (w d)")
                v_.scalar_tensor_tensor(rows, rows, wsel[0:P, bass.ds(t, 1)],
                                        x_sb[0:P, bass.ds(t, 1), :].rearrange("p w d -> p (w d)"), ALU.mult, ALU.add)\
                  .then_inc(rows_done, 1)


_INS = ("x", "src", "dst", "edge_type_8", "L0_gnn_conv_weights", "L0_gnn_attn_l", "L0_gnn_attn_r", "L0_gnn_h_bias",
        "L0_mix_w_qkv", "L0_mix_b_qkv", "L0_mix_kln_g", "L0_mix_kln_b", "L0_mix_vln_g", "L0_mix_vln_b", "L0_mix_w1",
        "L0_mix_b1", "L0_mix_w2", "L0_mix_b2", "L0_ffn_wr", "L0_ffn_br", "L0_ffn_w1", "L0_ffn_b1", "L0_ffn_w2",
        "L0_ffn_b2")


def kernel(**inputs):
    import concourse.bacc as bacc
    import numpy as np
    from concourse.bass_utils import run_bass_kernel_spmd

    nc = bacc.Bacc("TRN2", target_bir_lowering=False, num_devices=1)
    arrays = {name: np.ascontiguousarray(inputs[name]) for name in _INS}
    handles = {name: nc.dram_tensor(name, array.shape, mybir.dt.from_np(array.dtype), kind="ExternalInput").ap()
               for name, array in arrays.items()}
    out = nc.dram_tensor("out", (N, D), F32, kind="ExternalOutput").ap()
    graph_layer(nc, handles, out)
    result = run_bass_kernel_spmd(nc, [arrays], core_ids=[0])
    return result.results[0]["out"]
```
